# Optimizing a Trainium2 kernel written in Bass

```python
import numpy as np
import jax
import jax.numpy as jnp

def _softmax(x, axis=-1):
    return jax.nn.softmax(x, axis=axis)

def _gelu(x):
    return jax.nn.gelu(x, approximate=True)

def _silu(x):
    return jax.nn.silu(x)

def _sigmoid(x):
    return jax.nn.sigmoid(x)

def _layernorm(x, axis=-1, eps=1e-05):
    m = jnp.mean(x, axis=axis, keepdims=True)
    v = jnp.var(x, axis=axis, keepdims=True)
    return (x - m) / jnp.sqrt(v + eps)

def _scatter_add(tgt, idx, src, axis=0):
    return tgt.at[idx].add(src)

def _segment_sum(src, seg, n):
    return jax.ops.segment_sum(src, seg, n)
kernel_name = 'mk_flamingo_gated_d1_seqx_r8_0d9f3b'

def setup_inputs(seed: int=0):
    np.random.seed(seed)
    _w = jnp.asarray

    def _rec_inputs():
        import jax
        import jax.numpy as jnp
        _rk = jax.random.key(seed)
        x = 7.22e-05 + 1 * jax.random.normal(jax.random.fold_in(_rk, 1), (16, 64, 256), jnp.float32)
        _lenS = 64 - jax.random.randint(jax.random.fold_in(_rk, 7), (16,), 0, max(1, 64 // 4) + 1, jnp.int32)
        _lenS2 = 64 - jax.random.randint(jax.random.fold_in(_rk, 8), (16,), 0, max(1, 64 // 4) + 1, jnp.int32)
        _ctx_2048P = jax.random.normal(jax.random.fold_in(_rk, 11), (16, 16, 256), jnp.float32)
        _ctx_2048c = jax.random.dirichlet(jax.random.fold_in(_rk, 511), 0.3 * jnp.ones((16,), jnp.float32), (16, 64))
        _ctx_2048t = jnp.einsum('bsk,bkd->bsd', _ctx_2048c, _ctx_2048P)
        _ctx_2048t = _ctx_2048t * jax.lax.rsqrt(jnp.mean(jnp.square(_ctx_2048t)) + 1e-12) * 0.953939
        ctx_2048 = -0.000514642 + 1.00011 * (_ctx_2048t + 0.3 * jax.random.normal(jax.random.fold_in(_rk, 611), (16, 64, 256), jnp.float32))
        _g = jax.random.normal(jax.random.fold_in(_rk, 9001), (2, 1), jnp.float32)
        _g = jnp.sign(_g) * jnp.maximum(jnp.abs(_g), 1.0) + (_g == 0) * 1.0
        g_xattn = _g[0]
        g_ffn = _g[1]
        return (x, ctx_2048, g_xattn, g_ffn)
    x, ctx_2048, g_xattn, g_ffn = _rec_inputs()

    def _L0_xattn_setup():
        import jax, jax.numpy as jnp
        import numpy as np
        HIDDEN = 256
        NUM_HEADS = 16
        NUM_KV_HEADS = 4
        HEAD_DIM = 128
        ROPE_THETA = 10000.0
        EPS = 1e-06

        def rms_norm(x, w, eps=EPS):
            var = jnp.mean(jnp.square(x), axis=-1, keepdims=True)
            return x * jax.lax.rsqrt(var + eps) * w

        def rope_cache(L, head_dim, theta, dtype):
            inv_freq = 1.0 / theta ** (jnp.arange(0, head_dim, 2, dtype=jnp.float32) / head_dim)
            t = jnp.arange(L, dtype=jnp.float32)
            freqs = jnp.outer(t, inv_freq)
            emb = jnp.concatenate([freqs, freqs], -1)
            cos = jnp.cos(emb).astype(dtype)[None, :, None, :]
            sin = jnp.sin(emb).astype(dtype)[None, :, None, :]
            return (cos, sin)

        def rotate_half(x):
            x1, x2 = jnp.split(x, 2, axis=-1)
            return jnp.concatenate([-x2, x1], axis=-1)
        key = jax.random.key(seed)
        ks = jax.random.split(key, 10)
        B, L, T = (2, 256, 64)
        q_out = NUM_HEADS * HEAD_DIM
        kv_out = NUM_KV_HEADS * HEAD_DIM
        s = lambda fan_in: 1.0 / np.sqrt(fan_in)
        return {'x': jax.random.normal(ks[0], (B, L, HIDDEN), jnp.float32), 'h_ctx_kv': jax.random.normal(ks[1], (B, T, HIDDEN), jnp.float32), 'wq': jax.random.normal(ks[2], (HIDDEN, q_out), jnp.float32) * s(HIDDEN), 'wk': jax.random.normal(ks[3], (HIDDEN, kv_out), jnp.float32) * s(HIDDEN), 'wv': jax.random.normal(ks[4], (HIDDEN, kv_out), jnp.float32) * s(HIDDEN), 'wo': jax.random.normal(ks[5], (q_out, HIDDEN), jnp.float32) * s(q_out), 'wk_ctx': jax.random.normal(ks[6], (HIDDEN, kv_out), jnp.float32) * s(HIDDEN), 'wv_ctx': jax.random.normal(ks[7], (HIDDEN, kv_out), jnp.float32) * s(HIDDEN), 'q_norm_w': jnp.ones((HEAD_DIM,), jnp.float32), 'k_norm_w': jnp.ones((HEAD_DIM,), jnp.float32)}
    _L0_xattn_all = _L0_xattn_setup()
    _L0_xattn_in = {k: v for k, v in _L0_xattn_all.items() if k in ('wq', 'wk', 'wv', 'wo', 'wk_ctx', 'wv_ctx', 'q_norm_w', 'k_norm_w')}
    del _L0_xattn_all

    def _L0_ffn_setup():
        import jax, jax.numpy as jnp
        import numpy as np
        B, S, H, I = (1, 64, 256, 768)

        def _quantized_matmul(x, w, scale):
            wq = w.astype(jnp.float8_e4m3fn).astype(x.dtype)
            y = jnp.einsum('bsi,io->bso', x, wq)
            return y * scale
        key = jax.random.key(seed)
        ks = jax.random.split(key, 7)
        return {'x': jax.random.normal(ks[0], (B, S, H), dtype=jnp.float32), 'gate_w': jax.random.normal(ks[1], (H, I), dtype=jnp.float32) * 0.02, 'up_w': jax.random.normal(ks[2], (H, I), dtype=jnp.float32) * 0.02, 'down_w': jax.random.normal(ks[3], (I, H), dtype=jnp.float32) * 0.02, 'gate_scale': jax.random.uniform(ks[4], (I,), dtype=jnp.float32, minval=0.5, maxval=1.5), 'up_scale': jax.random.uniform(ks[5], (I,), dtype=jnp.float32, minval=0.5, maxval=1.5), 'down_scale': jax.random.uniform(ks[6], (H,), dtype=jnp.float32, minval=0.5, maxval=1.5)}
    _L0_ffn_all = _L0_ffn_setup()
    _L0_ffn_in = {k: v for k, v in _L0_ffn_all.items() if k in ('gate_w', 'up_w', 'down_w', 'gate_scale', 'up_scale', 'down_scale')}
    del _L0_ffn_all
    return {'x': x, 'ctx_2048': ctx_2048, 'g_xattn': g_xattn, 'g_ffn': g_ffn, 'L0_xattn_wq': _L0_xattn_in['wq'], 'L0_xattn_wk': _L0_xattn_in['wk'], 'L0_xattn_wv': _L0_xattn_in['wv'], 'L0_xattn_wo': _L0_xattn_in['wo'], 'L0_xattn_wk_ctx': _L0_xattn_in['wk_ctx'], 'L0_xattn_wv_ctx': _L0_xattn_in['wv_ctx'], 'L0_xattn_q_norm_w': _L0_xattn_in['q_norm_w'], 'L0_xattn_k_norm_w': _L0_xattn_in['k_norm_w'], 'L0_ffn_gate_w': _L0_ffn_in['gate_w'], 'L0_ffn_up_w': _L0_ffn_in['up_w'], 'L0_ffn_down_w': _L0_ffn_in['down_w'], 'L0_ffn_gate_scale': _L0_ffn_in['gate_scale'], 'L0_ffn_up_scale': _L0_ffn_in['up_scale'], 'L0_ffn_down_scale': _L0_ffn_in['down_scale']}

def reference(x, ctx_2048, g_xattn, g_ffn, L0_xattn_wq, L0_xattn_wk, L0_xattn_wv, L0_xattn_wo, L0_xattn_wk_ctx, L0_xattn_wv_ctx, L0_xattn_q_norm_w, L0_xattn_k_norm_w, L0_ffn_gate_w, L0_ffn_up_w, L0_ffn_down_w, L0_ffn_gate_scale, L0_ffn_up_scale, L0_ffn_down_scale):
    import jax
    import jax.numpy as jnp

    def _L0_xattn_ref(x, h_ctx_kv, wq, wk, wv, wo, wk_ctx, wv_ctx, q_norm_w, k_norm_w):
        import jax, jax.numpy as jnp
        import numpy as np
        HIDDEN = 256
        NUM_HEADS = 16
        NUM_KV_HEADS = 4
        HEAD_DIM = 128
        ROPE_THETA = 10000.0
        EPS = 1e-06

        def rms_norm(x, w, eps=EPS):
            var = jnp.mean(jnp.square(x), axis=-1, keepdims=True)
            return x * jax.lax.rsqrt(var + eps) * w

        def rope_cache(L, head_dim, theta, dtype):
            inv_freq = 1.0 / theta ** (jnp.arange(0, head_dim, 2, dtype=jnp.float32) / head_dim)
            t = jnp.arange(L, dtype=jnp.float32)
            freqs = jnp.outer(t, inv_freq)
            emb = jnp.concatenate([freqs, freqs], -1)
            cos = jnp.cos(emb).astype(dtype)[None, :, None, :]
            sin = jnp.sin(emb).astype(dtype)[None, :, None, :]
            return (cos, sin)

        def rotate_half(x):
            x1, x2 = jnp.split(x, 2, axis=-1)
            return jnp.concatenate([-x2, x1], axis=-1)
        B, L, _ = x.shape
        T = h_ctx_kv.shape[1]
        rep = NUM_HEADS // NUM_KV_HEADS
        q = (x @ wq).reshape(B, L, NUM_HEADS, HEAD_DIM)
        k = (x @ wk).reshape(B, L, NUM_KV_HEADS, HEAD_DIM)
        v = (x @ wv).reshape(B, L, NUM_KV_HEADS, HEAD_DIM)
        q = rms_norm(q, q_norm_w)
        k = rms_norm(k, k_norm_w)
        k_ctx = (h_ctx_kv @ wk_ctx).reshape(B, T, NUM_KV_HEADS, HEAD_DIM)
        v_ctx = (h_ctx_kv @ wv_ctx).reshape(B, T, NUM_KV_HEADS, HEAD_DIM)
        k_ctx = rms_norm(k_ctx, k_norm_w)
        cos, sin = rope_cache(L, HEAD_DIM, ROPE_THETA, x.dtype)
        q = q * cos + rotate_half(q) * sin
        k = k * cos + rotate_half(k) * sin
        k_full = jnp.concatenate([k_ctx, k], axis=1)
        v_full = jnp.concatenate([v_ctx, v], axis=1)
        k_full = jnp.repeat(k_full, rep, axis=2)
        v_full = jnpp_repeat = jnp.repeat(v_full, rep, axis=2)
        i = jnp.arange(L)[:, None]
        j = jnp.arange(L)[None, :]
        causal = jnp.where(j > i, -jnp.inf, 0.0).astype(x.dtype)
        mask = jnp.concatenate([jnp.zeros((L, T), x.dtype), causal], axis=1)
        scale = 1.0 / np.sqrt(HEAD_DIM)
        scores = jnp.einsum('blhd,bmhd->bhlm', q, k_full) * scale + mask
        probs = jax.nn.softmax(scores, axis=-1)
        out = jnp.einsum('bhlm,bmhd->blhd', probs, v_full)
        out = out.reshape(B, L, NUM_HEADS * HEAD_DIM)
        return out @ wo

    def _L0_ffn_ref(x, gate_w, up_w, down_w, gate_scale, up_scale, down_scale):
        import jax, jax.numpy as jnp
        import numpy as np
        B, S, H, I = (1, 64, 256, 768)

        def _quantized_matmul(x, w, scale):
            wq = w.astype(jnp.float8_e4m3fn).astype(x.dtype)
            y = jnp.einsum('bsi,io->bso', x, wq)
            return y * scale
        gate = jax.nn.silu(_quantized_matmul(x, gate_w, gate_scale))
        up = _quantized_matmul(x, up_w, up_scale)
        fuse = gate * up
        return _quantized_matmul(fuse, down_w, down_scale)
    x = x + jnp.tanh(g_xattn[0]) * _L0_xattn_ref(_layernorm(x, axis=-1), ctx_2048, L0_xattn_wq, L0_xattn_wk, L0_xattn_wv, L0_xattn_wo, L0_xattn_wk_ctx, L0_xattn_wv_ctx, L0_xattn_q_norm_w, L0_xattn_k_norm_w)
    x = x + jnp.tanh(g_ffn[0]) * _L0_ffn_ref(_layernorm(x, axis=-1), L0_ffn_gate_w, L0_ffn_up_w, L0_ffn_down_w, L0_ffn_gate_scale, L0_ffn_up_scale, L0_ffn_down_scale)
    return x

_drawn_inputs = setup_inputs


def setup_inputs(seed=0):
    import zlib

    import numpy as np

    out = dict(_drawn_inputs(seed))
    spreads = {'L0_xattn_q_norm_w': (1.0, 0.2), 'L0_xattn_k_norm_w': (1.0, 0.541)}
    factors = {'L0_ffn_gate_scale': 5.877, 'L0_ffn_up_scale': 6.804, 'L0_ffn_down_scale': 6.607}
    for name, (base, spread) in spreads.items():
        noise = np.random.default_rng([zlib.crc32(name.encode()), seed]).standard_normal(out[name].shape)
        drawn = base * np.exp(spread * noise) if base else spread * noise
        out[name] = jnp.asarray(drawn.astype(out[name].dtype))
    for name, factor in factors.items():
        out[name] = (out[name] * factor).astype(out[name].dtype)
    return out
```

```python
import math
from contextlib import ExitStack

import numpy as np

import concourse.bass as bass
from concourse import mybir

BATCHES, LEN, HID = 16, 64, 256
HEADS, GROUPS, DIM = 16, 4, 128
FF = 768
P = 128
TILES = BATCHES // 2
STEPS = TILES * GROUPS
HPG = HEADS // GROUPS
GW = HPG * DIM
KC = HID // P
FC = FF // P
HALF = DIM // 2

LN_EPS = 1e-5
RMS_EPS = 1e-6
MASKED = -1e30
FF_IN_SCALE = 64.0

E4M3_MIN_NORMAL = 2.0 ** -6
E4M3_ROUNDER = 1.5 * 2.0 ** 20
E4M3_OVERFLOW = 2.0 ** 120 / 460.0 * 256.0
EXPONENT_BITS = 0x7F800000

C_COS, C_SIN, C_MASK, C_ID, C_ALL = 0, DIM, 2 * DIM, 2 * DIM + LEN, 2 * DIM + LEN + P

KV_KINDS = ("k_ctx", "k_self", "v_ctx", "v_self")
CHUNKS = [("kv", 0), ("kv", 1), ("kv", 2), ("kv", 3), ("q", 0), ("q", 1), ("o", 0), ("gate", 0), ("q", 2), ("o", 1),
          ("gate", 1), ("q", 3), ("o", 2), ("up", 0), ("o", 3), ("up", 1), ("down", 0), ("down", 1)]
FF_CHUNKS = [c for c in CHUNKS if c[0] in ("gate", "up", "down")]
RING = 4
CHUNK_COLS = 1024

FIRST_STEP, LAST_STEP = -6, STEPS + 6


def build(nc, x, ctx_in, g_xattn, g_ffn, wq, wk, wv, wo, wk_ctx, wv_ctx, q_norm_w, k_norm_w,
          gate_w, up_w, down_w, gate_scale, up_scale, down_scale, constants, out):
    f32, f32r, f16, bf16, u32 = (mybir.dt.float32, mybir.dt.float32r, mybir.dt.float16, mybir.dt.bfloat16,
                                 mybir.dt.uint32)
    ALU, ACT, AX = mybir.AluOpType, mybir.ActivationFunctionType, mybir.AxisListType

    with ExitStack() as stack:
        def sb(name, shape, dt=f32):
            return stack.enter_context(nc.sbuf_tensor(name, shape, dt))

        def bank(name):
            return stack.enter_context(nc.psum_tensor(name, [P, 512], f32))

        def sem(name):
            return stack.enter_context(nc.semaphore(name))

        const = sb("const", [P, C_ALL])
        mask = sb("mask", [P, LEN], bf16)
        ident_bf = sb("ident_bf", [P, P], bf16)
        ident = const[:, C_ID:C_ID + P]
        minus_half = sb("minus_half", [P, HPG])
        rope = sb("rope", [P, 4, DIM])
        k_w_col = sb("k_w_col", [P, 1])
        gates = sb("gates", [P, 2])
        tanh_gates = sb("tanh_gates", [P, 2])
        ff_scales = sb("ff_scales", [P, 2, FC])
        tanh_scale = sb("tanh_scale", [P, FC])
        fuse_scale = sb("fuse_scale", [P, FC])
        down_rows = sb("down_rows", [P, HID])

        x_sb = sb("x_sb", [P, TILES, HID])
        ctx_sb = sb("ctx_sb", [P, 2, HID])
        xn = sb("xn", [P, HID])
        stage = sb("stage", [P, RING, CHUNK_COLS])
        w_kv = [sb(f"w_kv_{a}", [P, 4, KC, GW], f32r) for a in ("hi", "lo")]
        w_q = [sb(f"w_q_{a}", [P, GROUPS, KC, GW], f32r) for a in ("hi", "lo")]
        w_o = [sb(f"w_o_{a}", [P, GROUPS, HPG, HID], f32r) for a in ("hi", "lo")]
        w_ff = sb("w_ff", [P, 2, KC, FF], f16)
        w_down = sb("w_down", [P, FC, HID], f32r)
        quant_m = sb("quant_m", [P, FF])

        xt = [sb(f"xt_{a}", [P, 2, 2 * KC, P], f32r) for a in ("hi", "lo")]
        kt = sb("kt", [P, 2, GROUPS, 4, LEN])
        v_hi = sb("v_hi", [P, 2, 2, GW], f32r)
        v_lo = sb("v_lo", [P, 2, 2, GW], f32r)
        q_rot = sb("q_rot", [P, HPG, DIM])
        q_sin = sb("q_sin", [P, HPG, DIM])
        qt = sb("qt", [P, 2, HPG, LEN])
        k_cos = sb("k_cos", [P, HPG, DIM])
        k_sin = sb("k_sin", [P, HPG, DIM])
        kn = k_sin
        probs = sb("probs", [P, 4, P])
        pt_hi = sb("pt_hi", [P, 512], f32r)
        pt_lo = sb("pt_lo", [P, 512], f32r)
        ot_hi = sb("ot_hi", [P, HPG, P], f32r)
        ot_lo = sb("ot_lo", [P, HPG, P], f32r)
        squares = const[:, 0:2 * DIM].bitcast(bf16).rearrange("p (h d) -> p h d", h=HPG)

        ssq = sb("ssq", [P, HPG])
        ssq_rows = sb("ssq_rows", [P, 4])
        q_scale = sb("q_scale", [P, 2, 4])
        row_max = sb("row_max", [P, 4])
        exp_bias = sb("exp_bias", [P, 4])
        row_sum = sb("row_sum", [P, 4])
        row_inv = sb("row_inv", [P, 4])
        k_ssq = sb("k_ssq", [P, HPG])
        k_var = sb("k_var", [P, HPG])
        k_inv = sb("k_inv", [P, HPG])
        ln_stats = sb("ln_stats", [P, 6])
        ln_mean = sb("ln_mean", [P, 2])
        ln_var = sb("ln_var", [P, 1])
        ln_inv = sb("ln_inv", [P, 1])
        x2_stats = sb("x2_stats", [P, 6])
        x2_mean = sb("x2_mean", [P, 2])
        x2_var = sb("x2_var", [P, 1])
        x2_inv = sb("x2_inv", [P, 1])

        x1 = sb("x1", [P, 2, HID])
        x2n = xn
        x2t = [sb(f"x2t_{a}", [P, KC, P], f16) for a in ("hi", "lo")]
        tanh_g = sb("tanh_g", [P, 2, P])
        fuse = sb("fuse", [P, 2, P])
        fuse_hi = sb("fuse_hi", [P, FC, P], f32r)
        fuse_lo = sb("fuse_lo", [P, FC, P], f32r)
        down_y = fuse[:, :, :].rearrange("p a n -> p (a n)")

        ps_t, ps_q, ps_s, ps_o, ps_f, ps_k, ps_y, ps_p = (
            bank(n) for n in ("ps_transposed", "ps_q", "ps_scores", "ps_attn", "ps_ff", "ps_kv", "ps_y", "ps_probs"))

        const_in, small_in, x0_in, x_in = sem("const_in"), sem("small_in"), sem("x0_in"), sem("x_in")
        ctx_in_sem = [sem(f"ctx_in_{i}") for i in range(2)]
        chunk_in = [sem(f"chunk_in_{i}") for i in range(len(CHUNKS))]
        out_stored = [sem(f"out_stored_{i}") for i in range(2)]
        half_set = sem("half_set")
        tables_ready = sem("tables_ready")
        gates_ready = sem("gates_ready")
        w_hi_ready, w_lo_ready = sem("w_hi_ready"), sem("w_lo_ready")
        wo_hi_ready, wo_lo_ready = sem("wo_hi_ready"), sem("wo_lo_ready")
        quant_exp, quant_round, quant_sum, quant_diff, quant_nan, quant_done = (
            sem(n) for n in ("quant_exp", "quant_round", "quant_sum", "quant_diff", "quant_nan", "quant_done"))
        ln_counted, ln_averaged, ln_var_ready, ln_inv_ready, xn_ready = (
            sem(n) for n in ("ln_counted", "ln_averaged", "ln_var_ready", "ln_inv_ready", "xn_ready"))
        xc_turned, xt_hi_ready, xt_lo_ready = sem("xc_turned"), sem("xt_hi_ready"), sem("xt_lo_ready")
        kv_made = {kind: sem(f"{kind}_made") for kind in KV_KINDS}
        kc_squared, kc_var_ready, kc_inv_ready, kc_ready, kc_turned, kc_stored = (
            sem(n) for n in ("kc_squared", "kc_var_ready", "kc_inv_ready", "kc_ready", "kc_turned", "kc_stored"))
        ks_squared, ks_var_ready, ks_inv_ready, ks_roped, ks_added, ks_ready, ks_turned, ks_stored = (
            sem(n) for n in ("ks_squared", "ks_var_ready", "ks_inv_ready", "ks_roped", "ks_added", "ks_ready",
                             "ks_turned", "ks_stored"))
        vc_hi_ready, vc_lo_ready, vs_hi_ready, vs_lo_ready = (
            sem(n) for n in ("vc_hi_ready", "vc_lo_ready", "vs_hi_ready", "vs_lo_ready"))
        x1_ready, x2_counted, x2_averaged, x2_var_ready, x2_inv_ready, x2_ready, x2_turned, x2_hi_ready, x2_lo_ready = (
            sem(n) for n in ("x1_ready", "x2_counted", "x2_averaged", "x2_var_ready", "x2_inv_ready", "x2_ready",
                             "x2_turned", "x2_hi_ready", "x2_lo_ready"))
        ff_made, tanh_ready, gated_ready, fuse_ready, fuse_hi_ready, fuse_lo_ready = (
            sem(n) for n in ("ff_made", "tanh_ready", "gated_ready", "fuse_ready", "fuse_hi_ready", "fuse_lo_ready"))
        down_made, down_scaled, result_ready = sem("down_made"), sem("down_scaled"), sem("result_ready")
        q_made, q_squared, q_cos_ready, q_sin_ready, q_rot_ready, ssq_moved, q_scale_ready, q_turned, qt_ready = (
            sem(n) for n in ("q_made", "q_squared", "q_cos_ready", "q_sin_ready", "q_rot_ready", "ssq_moved",
                             "q_scale_ready", "q_turned", "qt_ready"))
        scores_made, max_ready, bias_ready, exp_ready, inv_ready, probs_ready, probs_turned, pt_hi_ready, pt_lo_ready = (
            sem(n) for n in ("scores_made", "max_ready", "bias_ready", "exp_ready", "inv_ready", "probs_ready",
                             "probs_turned", "pt_hi_ready", "pt_lo_ready"))
        attn_made, ot_hi_ready, ot_lo_ready, y_made = (
            sem(n) for n in ("attn_made", "ot_hi_ready", "ot_lo_ready", "y_made"))

        def step(u, k):
            return u * (2 * GROUPS) + k

        def tile(u, m):
            return u * 2 + m

        def is_step(u, k):
            return not isinstance(u, int) or 0 <= step(u, k) < STEPS

        def is_tile(u, m):
            return not isinstance(u, int) or 0 <= tile(u, m) < TILES

        def run_steps(eng, one_step):
            for k in range(FIRST_STEP, 2 * GROUPS):
                one_step(0, k)
            with eng.Fori(1, TILES // 2 - 1) as u:
                for k in range(2 * GROUPS):
                    one_step(u, k)
            last = TILES // 2 - 1
            for k in range(LAST_STEP - step(last, 0)):
                one_step(last, k)

        def four(ap):
            return ap[:, :].rearrange("p (h d) -> p h d", h=4)

        def rotated(ap):
            return ap.rearrange("p h (f j) -> p h f j", f=2)[:, :, ::-1, :]

        def halves(ap):
            return ap.rearrange("p h (f j) -> p h f j", f=2)

        def over_heads(row):
            return row.unsqueeze(1).broadcast_to([P, HPG, DIM])

        def staged(n, cols):
            return stage[:, n % RING, 0:cols]

        block = stack.enter_context(nc.Block())

        @block.sync
        def _(sp):
            x_by_half = x.rearrange("(t c) l n -> c l t n", c=2)
            out_by_half = out.rearrange("(t c) l n -> c l t n", c=2)
            ctx_rows = ctx_in.rearrange("(t c) l n -> (c l) t n", c=2)
            kv_views = [w.rearrange("(c p) n -> p c n", p=P) for w in (wk_ctx, wk, wv_ctx, wv)]
            wq_view = wq.rearrange("(c p) (g n) -> p g c n", p=P, g=GROUPS)
            wo_view = wo.rearrange("(g h p) n -> p g h n", p=P, g=GROUPS)
            ff_views = {"gate": gate_w, "up": up_w}
            down_view = down_w.rearrange("(p c) n -> p c n", p=P)

            def load_chunk(n):
                kind, i = CHUNKS[n]
                if n >= RING:
                    before = n - RING
                    kind_before, i_before = CHUNKS[before]
                    if kind_before == "o":
                        sp.wait_ge(wo_lo_ready, i_before + 1)
                    elif kind_before in ("kv", "q"):
                        sp.wait_ge(w_lo_ready, i_before + (kind_before == "q") * len(KV_KINDS) + 1)
                    else:
                        sp.wait_ge(quant_done, FF_CHUNKS.index(CHUNKS[before]) + 1)
                if kind == "kv":
                    sp.dma_start(staged(n, CHUNK_COLS).rearrange("p (c n) -> p c n", c=KC), kv_views[i])\
                      .then_inc(chunk_in[n], 16)
                elif kind == "q":
                    sp.dma_start(staged(n, CHUNK_COLS).rearrange("p (c n) -> p c n", c=KC), wq_view[:, i])\
                      .then_inc(chunk_in[n], 16)
                elif kind == "o":
                    sp.dma_start(staged(n, CHUNK_COLS).rearrange("p (h n) -> p h n", h=HPG), wo_view[:, i])\
                      .then_inc(chunk_in[n], 16)
                elif kind == "down":
                    sp.dma_start(staged(n, FF).rearrange("p (c n) -> p c n", c=FC // 2),
                                 down_view[:, i * (FC // 2):(i + 1) * (FC // 2), :]).then_inc(chunk_in[n], 16)
                else:
                    sp.dma_start(staged(n, FF), ff_views[kind][i * P:(i + 1) * P, :]).then_inc(chunk_in[n], 16)

            for r in range(2):
                sp.dma_start(x_sb[r * LEN:(r + 1) * LEN, 0, :], x_by_half[1 - r][:, 0, :]).then_inc(x0_in, 16)
            sp.dma_start(ctx_sb[:, 0, :], ctx_rows[:, 0, :]).then_inc(ctx_in_sem[0], 16)
            sp.dma_start(const[:, :], constants).then_inc(const_in, 16)
            load_chunk(0)
            load_chunk(1)
            for n, w in enumerate((q_norm_w, k_norm_w)):
                row = w.rearrange("(a d) -> a d", a=1)
                sp.dma_start(rope[:, 2 * n, :], row.broadcast_to([P, DIM])).then_inc(small_in, 16)
                for f in range(2):
                    sp.dma_start(rope[:, 2 * n + 1, f * HALF:(f + 1) * HALF],
                                 row[:, (1 - f) * HALF:(2 - f) * HALF].broadcast_to([P, HALF])).then_inc(small_in, 16)
            sp.dma_start(k_w_col[:, :], k_norm_w.rearrange("(d a) -> d a", a=1)).then_inc(small_in, 16)
            for n in range(2, RING):
                load_chunk(n)
            for n, w in enumerate((g_xattn, g_ffn)):
                sp.dma_start(gates[:, n:n + 1], w.rearrange("(a n) -> a n", a=1).broadcast_to([P, 1]))\
                  .then_inc(small_in, 16)
            for n, w in enumerate((gate_scale, up_scale)):
                sp.dma_start(ff_scales[:, n, :], w.rearrange("(p c) -> p c", p=P)).then_inc(small_in, 16)
            sp.dma_start(down_rows[:, :], down_scale.rearrange("(a n) -> a n", a=1).broadcast_to([P, HID]))\
              .then_inc(small_in, 16)
            sp.dma_start(ctx_sb[:, 1, :], ctx_rows[:, 1, :]).then_inc(ctx_in_sem[1], 16)
            for r in range(2):
                sp.dma_start(x_sb[r * LEN:(r + 1) * LEN, 1:TILES, :], x_by_half[1 - r][:, 1:TILES, :])\
                  .then_inc(x_in, 16)
            for n in range(RING, len(CHUNKS)):
                load_chunk(n)

            def store_tile(u, m):
                sp.wait_ge(result_ready, tile(u, m) + 1)
                for r in range(2):
                    sp.dma_start(out_by_half[1 - r][:, bass.ds(tile(u, m), 1), :],
                                 x1[r * LEN:(r + 1) * LEN, m % 2, :].unsqueeze(1)).then_inc(out_stored[m % 2], 16)

            def pair(u):
                for m in range(2):
                    if is_tile(u, m + 2):
                        sp.wait_ge(xc_turned, tile(u, m) + 1)
                        sp.dma_start(ctx_sb[:, m, :].unsqueeze(1), ctx_rows[:, bass.ds(tile(u, m + 2), 1), :])\
                          .then_inc(ctx_in_sem[m], 16)
                for m in range(2):
                    if is_tile(u, m - 2):
                        store_tile(u, m - 2)

            pair(0)
            with sp.Fori(1, TILES // 2 - 1) as u:
                pair(u)
            pair(TILES // 2 - 1)
            pair(TILES // 2)
            for m in range(2):
                sp.wait_ge(out_stored[m], 16 * 2 * (TILES // 2))

        @block.tensor
        def _(pe):
            def three_passes(dst, lhs, rhs, terms):
                n, passes = 0, [(0, 0), (0, 1), (1, 0)]
                for i in range(terms):
                    for a, b in passes:
                        last = nc.tensor.matmul(dst, lhs(a, i), rhs(b, i), start=(n == 0),
                                                stop=(n == 3 * terms - 1))
                        n += 1
                return last

            def turn(dst, srcs):
                for i, src in enumerate(srcs):
                    last = nc.tensor.matmul(dst[:, i * P:(i + 1) * P], src, ident, start=True, stop=True,
                                            is_transpose=True)
                return last

            def one_step(u, k):
                m, j = divmod(k, GROUPS)
                par, nxt = m % 2, (m + 1) % 2

                if is_step(u, k):
                    pe.wait_ge(q_rot_ready, step(u, k) + 1)
                    if j == 1 and is_tile(u, m + 1):
                        pe.wait_ge(xt_lo_ready, tile(u, m + 1) + 1)
                    if j == 2 and is_tile(u, m + 1):
                        pe.wait_ge(kc_stored, tile(u, m + 1) + 1)
                    if j == 3 and is_tile(u, m - 1):
                        pe.wait_ge(x2_lo_ready, tile(u, m - 1) + 1)
                    if j == 0:
                        pe.wait_ge(ks_stored, tile(u, m) + 1)
                    turn(ps_t, [q_rot[:, h, :] for h in range(HPG)]).then_inc(q_turned, 1)

                if is_step(u, k + 1):
                    g1 = (k + 1) % GROUPS
                    p1 = ((k + 1) // GROUPS) % 2
                    if isinstance(u, int) and 0 <= step(u, k + 1) < GROUPS:
                        pe.wait_ge(w_lo_ready, len(KV_KINDS) + step(u, k + 1) + 1)
                        pe.wait_ge(w_hi_ready, len(KV_KINDS) + step(u, k + 1) + 1)
                    pe.wait_ge(xt_lo_ready, tile(u, (k + 1) // GROUPS) + 1)
                    if is_step(u, k):
                        pe.wait_ge(q_squared, step(u, k) + 1)
                        pe.wait_ge(q_sin_ready, step(u, k) + 1)
                    three_passes(ps_q[:, :], lambda a, i: xt[a][:, p1, i, :], lambda b, i: w_q[b][:, g1, i, :], KC)\
                        .then_inc(q_made, 1)

                if is_step(u, k):
                    pe.wait_ge(qt_ready, step(u, k) + 1)
                if j == 0 and is_tile(u, m + 1):
                    pe.wait_ge(xn_ready, tile(u, m + 1) + 1)
                    if isinstance(u, int) and tile(u, m + 1) == 0:
                        pe.wait_ge(const_in, 16)
                    pe.wait_ge(ctx_in_sem[nxt], 16 * (u + (m + 1) // 2 + 1))
                    turn(ps_t, [xn[:, i * P:(i + 1) * P] for i in range(KC)]
                         + [ctx_sb[:, nxt, i * P:(i + 1) * P] for i in range(KC)]).then_inc(xc_turned, 1)
                if j == 1 and is_tile(u, m + 1):
                    pe.wait_ge(kc_ready, tile(u, m + 1) + 1)
                    turn(ps_t, [kn[:, h, :] for h in range(GROUPS)]).then_inc(kc_turned, 1)
                if j == 2 and is_tile(u, m - 1):
                    pe.wait_ge(x2_ready, tile(u, m - 1) + 1)
                    turn(ps_t, [x2n[:, i * P:(i + 1) * P] for i in range(KC)]).then_inc(x2_turned, 1)
                if j == 3 and is_tile(u, m + 1):
                    pe.wait_ge(ks_ready, tile(u, m + 1) + 1)
                    turn(ps_t, [kn[:, h, :] for h in range(GROUPS)]).then_inc(ks_turned, 1)

                if is_step(u, k):
                    if j == 0:
                        pe.wait_ge(ks_stored, tile(u, m) + 1)
                    if isinstance(u, int) and step(u, k) == 0:
                        pe.wait_ge(tables_ready, 6)
                    scores = four(ps_s)
                    for r in range(2):
                        nc.tensor.matmul(scores[:, 2 * r:2 * r + 2, r * LEN:(r + 1) * LEN], ident_bf[:, :],
                                         mask[:, :].unsqueeze(1).broadcast_to([P, 2, LEN]),
                                         start=(r == 0), stop=False, skip_group_check=True)
                    for r in range(2):
                        for pp in range(2):
                            last = nc.tensor.matmul(scores[:, 2 * r + pp, :],
                                                    qt[:, r, 2 * pp:2 * pp + 2, :],
                                                    kt[:, par, j, 2 * r:2 * r + 2, :],
                                                    start=False, stop=(r == 1 and pp == 1), skip_group_check=True)
                    last.then_inc(scores_made, 1)

                if is_step(u, k - 1):
                    g0, p0 = (k - 1) % GROUPS, ((k - 1) // GROUPS) % 2
                    pe.wait_ge(pt_lo_ready, step(u, k - 1) + 1)
                    if g0 == 0:
                        pe.wait_ge(vs_lo_ready, tile(u, (k - 1) // GROUPS) + 1)
                    for r in range(2):
                        v = (v_hi, v_lo)
                        pt = (pt_hi, pt_lo)
                        last = three_passes(ps_o[:, r * 256:(r + 1) * 256],
                                            lambda a, i: v[a][:, p0, r, g0 * DIM:(g0 + 1) * DIM],
                                            lambda b, i: pt[b][:, r * 256:(r + 1) * 256], 1)
                    last.then_inc(attn_made, 1)

                piece, ff_m = {2: (0, m - 1), 3: (1, m - 1), 0: (2, m - 2), 1: (None, m - 2)}[j]
                if is_tile(u, ff_m) and piece is not None:
                    pe.wait_ge(x2_lo_ready, tile(u, ff_m) + 1)
                    if isinstance(u, int) and tile(u, ff_m) == 0:
                        pe.wait_ge(quant_done, 4)
                    if piece > 0:
                        pe.wait_ge(fuse_ready, tile(u, ff_m) * 3 + piece)
                    elif is_tile(u, ff_m - 1):
                        pe.wait_ge(down_scaled, tile(u, ff_m))
                    for i, (w, c) in enumerate(((0, 2 * piece), (0, 2 * piece + 1), (1, 2 * piece), (1, 2 * piece + 1))):
                        n = 0
                        for kc in range(KC):
                            for a in range(2):
                                last = nc.tensor.matmul(ps_f[:, i * P:(i + 1) * P],
                                                        w_ff[:, w, kc, c * P:(c + 1) * P], x2t[a][:, kc, :],
                                                        start=(n == 0), stop=(n == 2 * KC - 1))
                                n += 1
                    last.then_inc(ff_made, 1)
                if is_tile(u, ff_m) and piece is None:
                    if isinstance(u, int) and tile(u, ff_m) == 0:
                        pe.wait_ge(quant_done, 6)
                    pe.wait_ge(fuse_ready, tile(u, ff_m) * 3 + 3)
                    pe.wait_ge(fuse_lo_ready, tile(u, ff_m) * 3 + 3)
                    for c in range(FC):
                        for a, part in enumerate((fuse_hi, fuse_lo)):
                            last = nc.tensor.matmul(ps_f[:, 0:HID], part[:, c, :], w_down[:, c, :],
                                                    start=(c == 0 and a == 0), stop=(c == FC - 1 and a == 1))
                    last.then_inc(down_made, 1)

                if is_tile(u, m + 1):
                    kind = KV_KINDS[j]
                    t1 = tile(u, m + 1)
                    pe.wait_ge(xt_lo_ready, t1 + 1)
                    if isinstance(u, int) and t1 == 0:
                        pe.wait_ge(w_hi_ready, j + 1)
                        pe.wait_ge(w_lo_ready, j + 1)
                    if j == 0 and is_tile(u, m):
                        pe.wait_ge(vs_lo_ready, t1)
                    if j == 1:
                        pe.wait_ge(kc_ready, t1 + 1)
                    if j == 2:
                        pe.wait_ge(ks_roped, t1 + 1)
                    if j == 3:
                        pe.wait_ge(vc_lo_ready, t1 + 1)
                    base = KC if kind.endswith("ctx") else 0
                    three_passes(ps_k[:, :], lambda a, i: xt[a][:, nxt, base + i, :], lambda b, i: w_kv[b][:, j, i, :],
                                 KC).then_inc(kv_made[kind], 1)

                if is_step(u, k - 1):
                    g0 = (k - 1) % GROUPS
                    m0 = (k - 1) // GROUPS
                    pe.wait_ge(ot_lo_ready, step(u, k - 1) + 1)
                    if isinstance(u, int) and 0 <= step(u, k - 1) < GROUPS:
                        pe.wait_ge(wo_lo_ready, g0 + 1)
                    if g0 == 0 and is_tile(u, m0 - 1):
                        pe.wait_ge(x1_ready, tile(u, m0))
                    ot = (ot_hi, ot_lo)
                    n = 0
                    for h in range(HPG):
                        for a, b in ((0, 0), (0, 1), (1, 0)):
                            last = nc.tensor.matmul(ps_y[:, 0:HID], ot[a][:, h, :], w_o[b][:, g0, h, :],
                                                    start=(g0 == 0 and n == 0),
                                                    stop=(g0 == GROUPS - 1 and n == 3 * HPG - 1))
                            n += 1
                    last.then_inc(y_made, 1)

                if is_step(u, k):
                    pe.wait_ge(probs_ready, step(u, k) + 1)
                    turn(ps_p, [probs[:, i, :] for i in range(4)]).then_inc(probs_turned, 1)

            run_steps(pe, one_step)

        @block.scalar
        def _(act):
            def weight_hi(kind, i):
                n = CHUNKS.index((kind, i))
                act.wait_ge(chunk_in[n], 16)
                dst = {"kv": w_kv, "q": w_q, "o": w_o}[kind][0]
                nc.scalar.activation(dst[:, i].rearrange("p c n -> p (c n)"), staged(n, CHUNK_COLS), ACT.Copy)\
                    .then_inc(wo_hi_ready if kind == "o" else w_hi_ready, 1)

            def square_heads(src, dst):
                for h in range(HPG):
                    last = nc.scalar.activation(squares[:, h, :], src[:, h * DIM:(h + 1) * DIM], ACT.Square,
                                                accum_out=dst[:, h:h + 1])
                return last

            def one_step(u, k):
                m, j = divmod(k, GROUPS)
                par, nxt = m % 2, (m + 1) % 2

                if isinstance(u, int) and -GROUPS <= step(u, k) < 0:
                    weight_hi("kv", j)
                    if j == GROUPS - 1:
                        weight_hi("q", 0)
                if isinstance(u, int) and 0 <= step(u, k) < GROUPS - 1:
                    weight_hi("q", step(u, k) + 1)

                if is_step(u, k):
                    act.wait_ge(q_turned, step(u, k) + 1)
                    nc.scalar.activation(qt[:, :, :, :], ps_t[:, :].rearrange("p (h r l) -> p r h l", h=HPG, r=2),
                                         ACT.Copy).then_inc(qt_ready, 1)

                if is_step(u, k + 1):
                    act.wait_ge(q_made, step(u, k + 1) + 1)
                    if is_step(u, k):
                        act.wait_ge(ssq_moved, step(u, k) + 1)
                        act.wait_ge(q_sin_ready, step(u, k) + 1)
                    if j == 1 and is_tile(u, m + 1):
                        act.wait_ge(kc_squared, tile(u, m + 1) + 1)
                    if j == 2 and is_tile(u, m + 1):
                        act.wait_ge(ks_squared, tile(u, m + 1) + 1)
                    square_heads(ps_q, ssq).then_inc(q_squared, 1)

                if j == 0 and is_tile(u, m + 1):
                    act.wait_ge(xc_turned, tile(u, m + 1) + 1)
                    nc.scalar.activation(xt[0][:, nxt, :, :], four(ps_t), ACT.Copy).then_inc(xt_hi_ready, 1)
                if j == 1 and is_tile(u, m + 1):
                    act.wait_ge(kc_turned, tile(u, m + 1) + 1)
                    nc.scalar.activation(kt[:, nxt, :, 2:0:-1, :],
                                         ps_t[:, :].rearrange("p (g c m) -> p g c m", g=GROUPS, c=2), ACT.Copy,
                                         scale=k_w_col[:, 0:1]).then_inc(kc_stored, 1)
                if j == 2 and is_tile(u, m - 1):
                    act.wait_ge(x2_turned, tile(u, m - 1) + 1)
                    nc.scalar.activation(x2t[0][:, :, :].rearrange("p c n -> p (c n)"), ps_t[:, 0:HID], ACT.Copy)\
                        .then_inc(x2_hi_ready, 1)
                if j == 3 and is_tile(u, m + 1):
                    act.wait_ge(ks_turned, tile(u, m + 1) + 1)
                    nc.scalar.activation(kt[:, nxt, :, 0:4:3, :],
                                         ps_t[:, :].rearrange("p (g c m) -> p g c m", g=GROUPS, c=2), ACT.Copy)\
                        .then_inc(ks_stored, 1)

                if is_step(u, k - 1):
                    act.wait_ge(attn_made, step(u, k - 1) + 1)
                    nc.scalar.activation(ot_hi[:, :, :].rearrange("p h (r l) -> p r h l", r=2),
                                         ps_o[:, :].rearrange("p (r h l) -> p r h l", r=2, h=HPG), ACT.Copy)\
                        .then_inc(ot_hi_ready, 1)

                if is_step(u, k):
                    act.wait_ge(bias_ready, step(u, k) + 1)
                    for i in range(4):
                        last = nc.scalar.activation(probs[:, i, :], ps_s[:, i * P:(i + 1) * P], ACT.Exp,
                                                    bias=exp_bias[:, i:i + 1], scale=q_scale[:, k % 2, i:i + 1],
                                                    accum_out=row_sum[:, i:i + 1])
                    last.then_inc(exp_ready, 1)

                piece, ff_m = {2: (0, m - 1), 3: (1, m - 1), 0: (2, m - 2), 1: (None, m - 2)}[j]
                if is_tile(u, ff_m) and piece is not None:
                    act.wait_ge(ff_made, tile(u, ff_m) * 3 + piece + 1)
                    if isinstance(u, int) and tile(u, ff_m) == 0 and piece == 0:
                        act.wait_ge(tables_ready, 8)
                    for i in range(2):
                        c = 2 * piece + i
                        last = nc.scalar.activation(tanh_g[:, i, :], ps_f[:, i * P:(i + 1) * P], ACT.Tanh,
                                                    scale=tanh_scale[:, c:c + 1])
                    last.then_inc(tanh_ready, 1)

                if is_tile(u, ff_m) and piece is not None:
                    act.wait_ge(fuse_ready, tile(u, ff_m) * 3 + piece + 1)
                    nc.scalar.activation(fuse_hi[:, 2 * piece:2 * piece + 2, :], fuse[:, :, :], ACT.Copy)\
                        .then_inc(fuse_hi_ready, 1)

                if is_tile(u, m + 1):
                    t1 = tile(u, m + 1)
                    act.wait_ge(kv_made[KV_KINDS[j]], t1 + 1)
                    if j in (0, 1) and is_step(u, k + 1):
                        act.wait_ge(q_squared, step(u, k + 1) + 1)
                    if j == 0:
                        if isinstance(u, int) and t1 == 0:
                            act.wait_ge(tables_ready, 6)
                        if is_tile(u, m):
                            act.wait_ge(ks_var_ready, t1)
                        square_heads(ps_k, k_ssq).then_inc(kc_squared, 1)
                    if j == 1:
                        act.wait_ge(kc_var_ready, t1 + 1)
                        square_heads(ps_k, k_ssq).then_inc(ks_squared, 1)
                    if j == 2:
                        for c in range(2):
                            last = nc.scalar.activation(v_hi[c * LEN:(c + 1) * LEN, nxt, 1 - c, :],
                                                        ps_k[c * LEN:(c + 1) * LEN, :], ACT.Copy)
                        last.then_inc(vc_hi_ready, 1)
                    if j == 3:
                        for r in range(2):
                            last = nc.scalar.activation(v_hi[r * LEN:(r + 1) * LEN, nxt, r, :],
                                                        ps_k[r * LEN:(r + 1) * LEN, :], ACT.Copy)
                        last.then_inc(vs_hi_ready, 1)

                if isinstance(u, int) and 0 <= step(u, k) < GROUPS:
                    weight_hi("o", step(u, k))
                if isinstance(u, int) and step(u, k) == -1:
                    act.wait_ge(small_in, 16 * 12)
                    nc.scalar.activation(tanh_gates[:, :], gates[:, :], ACT.Tanh).then_inc(gates_ready, 1)

                if is_step(u, k):
                    act.wait_ge(probs_turned, step(u, k) + 1)
                    nc.scalar.activation(pt_hi[:, :], ps_p[:, :], ACT.Copy).then_inc(pt_hi_ready, 1)

            run_steps(act, one_step)

        @block.vector
        def _(dve):
            def as_f32(ap):
                return ap.bitcast(f32)

            def weight_lo(kind, i):
                n = CHUNKS.index((kind, i))
                dve.wait_ge(w_hi_ready, i + (kind == "q") * len(KV_KINDS) + 1)
                hi, lo = {"kv": w_kv, "q": w_q}[kind]
                nc.vector.tensor_tensor(lo[:, i].rearrange("p c n -> p (c n)"), staged(n, CHUNK_COLS),
                                        as_f32(hi[:, i].rearrange("p c n -> p (c n)")), ALU.subtract)\
                    .then_inc(w_lo_ready, 1)

            def quantize_first(i):
                n = CHUNKS.index(FF_CHUNKS[i])
                dve.wait_ge(chunk_in[n], 16)
                if i:
                    dve.wait_ge(quant_done, i)
                nc.vector.tensor_scalar(quant_m[:, :].bitcast(u32), staged(n, FF).bitcast(u32), EXPONENT_BITS, None,
                                        ALU.bitwise_and).then_inc(quant_exp, 1)
                dve.wait_ge(quant_exp, i + 1)
                nc.vector.tensor_scalar(quant_m[:, :], quant_m[:, :], E4M3_MIN_NORMAL, E4M3_ROUNDER,
                                        ALU.max, ALU.mult).then_inc(quant_round, 1)

            def quantize_last(i):
                n = CHUNKS.index(FF_CHUNKS[i])
                dve.wait_ge(quant_diff, i + 1)
                nc.vector.tensor_scalar(quant_m[:, :], staged(n, FF), E4M3_OVERFLOW, 0.0, ALU.mult, ALU.mult)\
                    .then_inc(quant_nan, 1)

            def tables():
                dve.wait_ge(const_in, 16)
                nc.vector.tensor_copy(mask[:, :], const[:, C_MASK:C_MASK + LEN]).then_inc(tables_ready, 1)
                nc.vector.tensor_copy(ident_bf[:, :], ident).then_inc(tables_ready, 1)
                dve.wait_ge(small_in, 16 * 12)
                for n in range(4):
                    col = C_COS if n % 2 == 0 else C_SIN
                    nc.vector.tensor_tensor(rope[:, n, :], const[:, col:col + DIM], rope[:, n, :], ALU.mult)\
                        .then_inc(tables_ready, 1)
                nc.vector.tensor_scalar(tanh_scale[:, :], ff_scales[:, 0, :], 0.5 / FF_IN_SCALE, None, ALU.mult)\
                    .then_inc(tables_ready, 1)
                nc.vector.scalar_tensor_tensor(fuse_scale[:, :], ff_scales[:, 0, :], 0.5 / FF_IN_SCALE ** 2,
                                               ff_scales[:, 1, :], ALU.mult, ALU.mult).then_inc(tables_ready, 1)

            def down_row_scale():
                dve.wait_ge(gates_ready, 1)
                nc.vector.tensor_scalar(down_rows[:, :], down_rows[:, :], tanh_gates[:, 1:2], None, ALU.mult)\
                    .then_inc(tables_ready, 1)

            def x_tile(u, m):
                if isinstance(u, int):
                    return x_sb[:, tile(u, m), :]
                return x_sb[:, bass.ds(tile(u, m), 1), :].rearrange("p a n -> p (a n)")

            def one_step(u, k):
                m, j = divmod(k, GROUPS)
                par, nxt = m % 2, (m + 1) % 2

                if isinstance(u, int) and -GROUPS <= step(u, k) < 0:
                    weight_lo("kv", j)
                if isinstance(u, int) and -1 <= step(u, k) < GROUPS - 1:
                    weight_lo("q", step(u, k) + 1)

                if j == 1 and is_tile(u, m + 1):
                    dve.wait_ge(kc_inv_ready, tile(u, m + 1) + 1)
                    if is_tile(u, m):
                        dve.wait_ge(ks_turned, tile(u, m) + 1)
                    nc.vector.tensor_tensor(kn[:, :, :], four(ps_k), k_inv[:, :].unsqueeze(2).broadcast_to([P, HPG, DIM]),
                                            ALU.mult).then_inc(kc_ready, 1)
                if j == 3 and is_tile(u, m + 2):
                    dve.wait_ge(ln_inv_ready, tile(u, m + 2) + 1)
                    if is_tile(u, m + 1):
                        dve.wait_ge(xc_turned, tile(u, m + 1) + 1)
                    if is_tile(u, m - 1):
                        dve.wait_ge(x2_turned, tile(u, m - 1) + 1)
                    nc.vector.tensor_scalar(xn[:, :], x_tile(u, m + 2), ln_mean[:, 0:1], ln_inv[:, 0:1],
                                            ALU.subtract, ALU.mult).then_inc(xn_ready, 1)

                ln_now = j == 2 and is_tile(u, m + 2)
                ln_count = tile(u, m + 2) + 1
                if ln_now:
                    if isinstance(u, int) and tile(u, m + 2) == 0:
                        dve.wait_ge(x0_in, 32)
                    if isinstance(u, int) and tile(u, m + 2) == 1:
                        dve.wait_ge(x_in, 32)
                    nc.vector.bn_stats(ln_stats[:, :], x_tile(u, m + 2)).then_inc(ln_counted, 1)
                    dve.wait_ge(ln_counted, ln_count)

                if is_step(u, k):
                    dve.wait_ge(scores_made, step(u, k) + 1)
                    nc.vector.tensor_reduce(row_max[:, :], four(ps_s), AX.X, ALU.max).then_inc(max_ready, 1)
                    dve.wait_ge(max_ready, step(u, k) + 1)
                    dve.wait_ge(q_scale_ready, step(u, k) + 1)
                    nc.vector.scalar_tensor_tensor(exp_bias[:, :], row_max[:, :], -1.0, q_scale[:, k % 2, :],
                                                   ALU.mult, ALU.mult).then_inc(bias_ready, 1)

                if ln_now:
                    nc.vector.bn_aggr(ln_mean[:, :], ln_stats[:, :]).then_inc(ln_averaged, 1)
                    dve.wait_ge(ln_averaged, ln_count)
                    if is_tile(u, m + 1):
                        dve.wait_ge(ln_inv_ready, ln_count - 1)
                    nc.vector.tensor_scalar(ln_var[:, :], ln_mean[:, 1:2], LN_EPS, None, ALU.add).then_inc(ln_var_ready, 1)

                if j == 0 and is_tile(u, m + 1):
                    dve.wait_ge(xt_hi_ready, tile(u, m + 1) + 1)
                    nc.vector.tensor_tensor(xt[1][:, nxt, :, :], four(ps_t), as_f32(xt[0][:, nxt, :, :]), ALU.subtract)\
                        .then_inc(xt_lo_ready, 1)
                if j == 2 and is_tile(u, m - 1):
                    dve.wait_ge(x2_hi_ready, tile(u, m - 1) + 1)
                    nc.vector.tensor_tensor(x2t[1][:, :, :].rearrange("p c n -> p (c n)"), ps_t[:, 0:HID],
                                            x2t[0][:, :, :].rearrange("p c n -> p (c n)"), ALU.subtract)\
                        .then_inc(x2_lo_ready, 1)

                if isinstance(u, int) and step(u, k) == -GROUPS:
                    tables()

                if is_step(u, k + 1):
                    dve.wait_ge(q_squared, step(u, k + 1) + 1)
                    if is_step(u, k):
                        dve.wait_ge(q_turned, step(u, k) + 1)
                    nc.vector.tensor_tensor(q_rot[:, :, :], four(ps_q), over_heads(rope[:, 0, :]), ALU.mult)\
                        .then_inc(q_cos_ready, 1)

                if is_step(u, k - 1):
                    dve.wait_ge(ot_hi_ready, step(u, k - 1) + 1)
                    nc.vector.tensor_tensor(ot_lo[:, :, :].rearrange("p h (r l) -> p r h l", r=2),
                                            ps_o[:, :].rearrange("p (r h l) -> p r h l", r=2, h=HPG),
                                            as_f32(ot_hi[:, :, :]).rearrange("p h (r l) -> p r h l", r=2), ALU.subtract)\
                        .then_inc(ot_lo_ready, 1)

                if is_step(u, k + 1):
                    nc.vector.tensor_tensor(halves(q_sin[:, :, :]), rotated(four(ps_q)), halves(over_heads(rope[:, 1, :])),
                                            ALU.mult).then_inc(q_sin_ready, 1)
                    if is_step(u, k):
                        dve.wait_ge(q_scale_ready, step(u, k) + 1)
                    for r in range(2):
                        for hh in range(2):
                            last = nc.vector.tensor_scalar(ssq_rows[hh * LEN:(hh + 1) * LEN, 2 * r:2 * r + 2],
                                                           ssq[r * LEN:(r + 1) * LEN, hh::2], DIM * RMS_EPS, None,
                                                           ALU.add)
                    last.then_inc(ssq_moved, 1)

                if is_step(u, k):
                    dve.wait_ge(exp_ready, step(u, k) + 1)
                    nc.vector.reciprocal(row_inv[:, :], row_sum[:, :]).then_inc(inv_ready, 1)
                    dve.wait_ge(inv_ready, step(u, k) + 1)
                    for i in range(4):
                        last = nc.vector.tensor_scalar(probs[:, i, :], probs[:, i, :], row_inv[:, i:i + 1], None, ALU.mult)
                    last.then_inc(probs_ready, 1)

                piece, ff_m = {2: (0, m - 1), 3: (1, m - 1), 0: (2, m - 2), 1: (None, m - 2)}[j]
                if is_tile(u, ff_m) and piece is not None:
                    count = tile(u, ff_m) * 3 + piece + 1
                    dve.wait_ge(tanh_ready, count)
                    nc.vector.scalar_tensor_tensor(tanh_g[:, :, :].rearrange("p a n -> p (a n)"),
                                                   tanh_g[:, :, :].rearrange("p a n -> p (a n)"), 1.0,
                                                   ps_f[:, 0:2 * P], ALU.add, ALU.mult).then_inc(gated_ready, 1)
                    dve.wait_ge(gated_ready, count)
                    if piece > 0:
                        dve.wait_ge(fuse_lo_ready, count - 1)
                    elif is_tile(u, ff_m - 1):
                        dve.wait_ge(result_ready, tile(u, ff_m))
                    for i in range(2):
                        c = 2 * piece + i
                        last = nc.vector.scalar_tensor_tensor(fuse[:, i, :], tanh_g[:, i, :], fuse_scale[:, c:c + 1],
                                                              ps_f[:, (2 + i) * P:(3 + i) * P], ALU.mult, ALU.mult)
                    last.then_inc(fuse_ready, 1)
                if is_tile(u, ff_m) and piece is None:
                    dve.wait_ge(down_made, tile(u, ff_m) + 1)
                    dve.wait_ge(fuse_lo_ready, tile(u, ff_m) * 3 + 3)
                    nc.vector.tensor_tensor(down_y, ps_f[:, 0:HID], down_rows[:, :], ALU.mult)\
                        .then_inc(down_scaled, 1)

                if is_tile(u, m + 1):
                    t1 = tile(u, m + 1)
                    if j == 0:
                        dve.wait_ge(kc_squared, t1 + 1)
                        if is_tile(u, m):
                            dve.wait_ge(ks_inv_ready, t1)
                        nc.vector.tensor_scalar(k_var[:, :], k_ssq[:, :], 1.0 / DIM, RMS_EPS, ALU.mult, ALU.add)\
                            .then_inc(kc_var_ready, 1)
                    if j == 1:
                        dve.wait_ge(ks_squared, t1 + 1)
                        nc.vector.tensor_scalar(k_var[:, :], k_ssq[:, :], 1.0 / DIM, RMS_EPS, ALU.mult, ALU.add)\
                            .then_inc(ks_var_ready, 1)
                        dve.wait_ge(kc_turned, t1 + 1)
                        nc.vector.tensor_tensor(k_cos[:, :, :], four(ps_k), over_heads(rope[:, 2, :]), ALU.mult)
                        nc.vector.tensor_tensor(halves(k_sin[:, :, :]), rotated(four(ps_k)),
                                                halves(over_heads(rope[:, 3, :])), ALU.mult).then_inc(ks_roped, 1)
                    if j == 2:
                        dve.wait_ge(vc_hi_ready, t1 + 1)
                        for c in range(2):
                            rows = slice(c * LEN, (c + 1) * LEN)
                            last = nc.vector.tensor_tensor(v_lo[rows, nxt, 1 - c, :], ps_k[rows, :],
                                                           as_f32(v_hi[rows, nxt, 1 - c, :]), ALU.subtract)
                        last.then_inc(vc_lo_ready, 1)
                    if j == 3:
                        dve.wait_ge(vs_hi_ready, t1 + 1)
                        for r in range(2):
                            rows = slice(r * LEN, (r + 1) * LEN)
                            last = nc.vector.tensor_tensor(v_lo[rows, nxt, r, :], ps_k[rows, :],
                                                           as_f32(v_hi[rows, nxt, r, :]), ALU.subtract)
                        last.then_inc(vs_lo_ready, 1)

                if j == 0 and is_tile(u, m - 1):
                    count = tile(u, m - 1) + 1
                    dve.wait_ge(y_made, step(u, k - 1) + 1)
                    if is_tile(u, m - 3):
                        dve.wait_ge(out_stored[nxt], (u + (m - 3) // 2 + 1) * 32)
                    nc.vector.scalar_tensor_tensor(x1[:, nxt, :], ps_y[:, 0:HID], tanh_gates[:, 0:1], x_tile(u, m - 1),
                                                   ALU.mult, ALU.add).then_inc(x1_ready, 1)
                    dve.wait_ge(x1_ready, count)
                    nc.vector.bn_stats(x2_stats[:, :], x1[:, nxt, :]).then_inc(x2_counted, 1)
                    dve.wait_ge(x2_counted, count)
                if j == 1 and is_tile(u, m - 1):
                    dve.wait_ge(x2_inv_ready, tile(u, m - 1) + 1)
                    if is_tile(u, m + 1):
                        dve.wait_ge(xc_turned, tile(u, m + 1) + 1)
                    nc.vector.tensor_scalar(x2n[:, :], x1[:, nxt, :], x2_mean[:, 0:1], x2_inv[:, 0:1],
                                            ALU.subtract, ALU.mult).then_inc(x2_ready, 1)

                if isinstance(u, int) and step(u, k) == 0:
                    down_row_scale()
                if isinstance(u, int) and 0 <= step(u, k) < 6:
                    quantize_first(step(u, k))

                if is_step(u, k):
                    dve.wait_ge(pt_hi_ready, step(u, k) + 1)
                    nc.vector.tensor_tensor(pt_lo[:, :], ps_p[:, :], as_f32(pt_hi[:, :]), ALU.subtract)\
                        .then_inc(pt_lo_ready, 1)

                if j == 0 and is_tile(u, m - 1):
                    count = tile(u, m - 1) + 1
                    nc.vector.bn_aggr(x2_mean[:, :], x2_stats[:, :]).then_inc(x2_averaged, 1)
                    dve.wait_ge(x2_averaged, count)
                    if is_tile(u, m - 2):
                        dve.wait_ge(x2_inv_ready, count - 1)
                    nc.vector.tensor_scalar(x2_var[:, :], x2_mean[:, 1:2], LN_EPS, FF_IN_SCALE ** -2, ALU.add, ALU.mult)\
                        .then_inc(x2_var_ready, 1)

                if isinstance(u, int) and 0 <= step(u, k) < 6:
                    quantize_last(step(u, k))

            run_steps(dve, one_step)

        @block.gpsimd
        def _(pool):
            def inverse_root(dst, src):
                return nc.gpsimd.tensor_tensor(dst, src, minus_half[:, 0:src.shape[1]], ALU.pow)

            def wo_lo(g):
                n = CHUNKS.index(("o", g))
                pool.wait_ge(wo_hi_ready, g + 1)
                nc.gpsimd.tensor_tensor(w_o[1][:, g].rearrange("p h n -> p (h n)"), staged(n, CHUNK_COLS),
                                        w_o[0][:, g].rearrange("p h n -> p (h n)").bitcast(f32), ALU.subtract)\
                    .then_inc(wo_lo_ready, 1)

            def quantize_round(i):
                n = CHUNKS.index(FF_CHUNKS[i])
                pool.wait_ge(quant_round, i + 1)
                nc.gpsimd.tensor_tensor(staged(n, FF), staged(n, FF), quant_m[:, :], ALU.add).then_inc(quant_sum, 1)
                pool.wait_ge(quant_sum, i + 1)
                nc.gpsimd.tensor_tensor(staged(n, FF), staged(n, FF), quant_m[:, :], ALU.subtract)\
                    .then_inc(quant_diff, 1)

            def quantize_store(i):
                kind, c = FF_CHUNKS[i]
                pool.wait_ge(quant_nan, i + 1)
                if kind == "down":
                    dst = w_down[:, c * (FC // 2):(c + 1) * (FC // 2), :].rearrange("p c n -> p (c n)")
                else:
                    dst = w_ff[:, ("gate", "up").index(kind), c, :].rearrange("k (c p) -> k p c", c=FC)
                rounded, nans = staged(CHUNKS.index(FF_CHUNKS[i]), FF), quant_m[:, :]
                if kind != "down":
                    rounded, nans = (a.rearrange("k (p c) -> k p c", c=FC) for a in (rounded, nans))
                nc.gpsimd.tensor_tensor(dst, rounded, nans, ALU.add).then_inc(quant_done, 1)

            def one_step(u, k):
                m, j = divmod(k, GROUPS)

                if is_step(u, k + 1):
                    pool.wait_ge(q_sin_ready, step(u, k + 1) + 1)
                    nc.gpsimd.tensor_tensor(q_rot[:, :, :], q_rot[:, :, :], q_sin[:, :, :], ALU.add)\
                        .then_inc(q_rot_ready, 1)
                    pool.wait_ge(ssq_moved, step(u, k + 1) + 1)
                    if is_step(u, k - 1):
                        pool.wait_ge(exp_ready, step(u, k - 1) + 1)
                    inverse_root(q_scale[:, (k + 1) % 2, :], ssq_rows[:, :]).then_inc(q_scale_ready, 1)

                piece, ff_m = {2: (0, m - 1), 3: (1, m - 1), 0: (2, m - 2), 1: (None, m - 2)}[j]
                if is_tile(u, ff_m) and piece is not None:
                    count = tile(u, ff_m) * 3 + piece + 1
                    hi = fuse_hi[:, 2 * piece:2 * piece + 2, :]
                    pool.wait_ge(fuse_hi_ready, count)
                    nc.gpsimd.tensor_tensor(fuse_lo[:, 2 * piece:2 * piece + 2, :], fuse[:, :, :], hi.bitcast(f32),
                                            ALU.subtract).then_inc(fuse_lo_ready, 1)
                if is_tile(u, ff_m) and piece is None:
                    pool.wait_ge(down_scaled, tile(u, ff_m) + 1)
                    nc.gpsimd.tensor_tensor(x1[:, m % 2, :], down_y, x1[:, m % 2, :], ALU.add)\
                        .then_inc(result_ready, 1)

                if is_tile(u, m + 1):
                    t1 = tile(u, m + 1)
                    if j == 0:
                        pool.wait_ge(kc_var_ready, t1 + 1)
                        if is_tile(u, m):
                            pool.wait_ge(ks_ready, t1)
                        inverse_root(k_inv[:, :], k_var[:, :]).then_inc(kc_inv_ready, 1)
                    if j == 1:
                        pool.wait_ge(ks_var_ready, t1 + 1)
                        pool.wait_ge(kc_ready, t1 + 1)
                        inverse_root(k_inv[:, :], k_var[:, :]).then_inc(ks_inv_ready, 1)
                        pool.wait_ge(ks_roped, t1 + 1)
                        nc.gpsimd.tensor_tensor(k_cos[:, :, :], k_cos[:, :, :], k_sin[:, :, :], ALU.add)\
                            .then_inc(ks_added, 1)
                        pool.wait_ge(ks_added, t1 + 1)
                        pool.wait_ge(ks_inv_ready, t1 + 1)
                        nc.gpsimd.tensor_tensor(kn[:, :, :], k_cos[:, :, :],
                                                k_inv[:, :].unsqueeze(2).broadcast_to([P, HPG, DIM]), ALU.mult)\
                            .then_inc(ks_ready, 1)

                if j == 2 and is_tile(u, m + 2):
                    pool.wait_ge(ln_var_ready, tile(u, m + 2) + 1)
                    if is_tile(u, m + 1):
                        pool.wait_ge(xn_ready, tile(u, m + 1) + 1)
                    inverse_root(ln_inv[:, :], ln_var[:, :]).then_inc(ln_inv_ready, 1)
                if j == 0 and is_tile(u, m - 1):
                    pool.wait_ge(x2_var_ready, tile(u, m - 1) + 1)
                    if is_tile(u, m - 2):
                        pool.wait_ge(x2_ready, tile(u, m - 2) + 1)
                    inverse_root(x2_inv[:, :], x2_var[:, :]).then_inc(x2_inv_ready, 1)

                if isinstance(u, int) and 0 <= step(u, k) < GROUPS:
                    wo_lo(step(u, k))
                if isinstance(u, int) and 0 <= step(u, k) < 6:
                    quantize_round(step(u, k))
                    quantize_store(step(u, k))

            nc.gpsimd.memset(minus_half[:, :], -0.5).then_inc(half_set, 1)
            pool.wait_ge(half_set, 1)
            run_steps(pool, one_step)


_INS = ["x", "ctx_2048", "g_xattn", "g_ffn", "L0_xattn_wq", "L0_xattn_wk", "L0_xattn_wv", "L0_xattn_wo",
        "L0_xattn_wk_ctx", "L0_xattn_wv_ctx", "L0_xattn_q_norm_w", "L0_xattn_k_norm_w", "L0_ffn_gate_w",
        "L0_ffn_up_w", "L0_ffn_down_w", "L0_ffn_gate_scale", "L0_ffn_up_scale", "L0_ffn_down_scale"]


def shape_constants():
    inv_freq = (1.0 / 10000.0 ** (np.arange(0, DIM, 2, dtype=np.float32) / DIM)).astype(np.float32)
    angles = np.outer(np.arange(LEN, dtype=np.float32), inv_freq)
    angles = np.concatenate([angles, angles], -1)
    sign = np.where(np.arange(DIM) < HALF, -1.0, 1.0).astype(np.float32)
    table = np.zeros((P, C_ALL), np.float32)
    table[:, C_COS:C_COS + DIM] = np.tile(np.cos(angles), (2, 1))
    table[:, C_SIN:C_SIN + DIM] = np.tile(np.sin(angles) * sign, (2, 1))
    late = np.arange(LEN)[None, :] > np.arange(LEN)[:, None]
    table[:, C_MASK:C_MASK + LEN] = np.tile(np.where(late, MASKED, 0.0), (2, 1))
    table[:, C_ID:C_ID + P] = np.eye(P)
    return table


def kernel(**inputs):
    import concourse.bacc as bacc
    from concourse.bass_utils import run_bass_kernel_spmd

    nc = bacc.Bacc("TRN2", target_bir_lowering=False, num_devices=1)
    arrays, args = {}, []
    given = [(name, np.ascontiguousarray(inputs[name])) for name in _INS] + [("constants", shape_constants())]
    for name, a in given:
        arrays[f"in_{name}_dram"] = a
        args.append(nc.dram_tensor(f"in_{name}_dram", a.shape, mybir.dt.from_np(a.dtype), kind="ExternalInput").ap())
    args.append(nc.dram_tensor("out_0_dram", (BATCHES, LEN, HID), mybir.dt.float32, kind="ExternalOutput").ap())
    build(nc, *args)
    r = run_bass_kernel_spmd(nc, [arrays], core_ids=[0])
    return r.results[0]["out_0_dram"]
```

```python
import math
from contextlib import ExitStack

import numpy as np

import concourse.bass as bass
from concourse import mybir

BATCHES, LEN, HID = 16, 64, 256
HEADS, GROUPS, DIM = 16, 4, 128
FF = 768
P = 128
TILES = BATCHES // 2
STEPS = TILES * GROUPS
HPG = HEADS // GROUPS
GW = HPG * DIM
KC = HID // P
FC = FF // P
HALF = DIM // 2

LN_EPS = 1e-5
RMS_EPS = 1e-6
MASKED = -1e30
FF_IN_SCALE = 64.0

E4M3_MIN_NORMAL = 2.0 ** -6
E4M3_ROUNDER = 1.5 * 2.0 ** 20
E4M3_OVERFLOW = 2.0 ** 120 / 460.0 * 256.0
EXPONENT_BITS = 0x7F800000

C_COS, C_SIN, C_MASK, C_ID, C_ALL = 0, DIM, 2 * DIM, 2 * DIM + LEN, 2 * DIM + LEN + P

KV_KINDS = ("k_ctx", "k_self", "v_ctx", "v_self")
CHUNKS = [("kv", 0), ("kv", 1), ("kv", 2), ("kv", 3), ("q", 0), ("q", 1), ("q", 2), ("o", 0), ("q", 3), ("gate", 0),
          ("o", 1), ("gate", 1), ("o", 2), ("up", 0), ("o", 3), ("up", 1), ("down", 0), ("down", 1)]
FF_CHUNKS = [c for c in CHUNKS if c[0] in ("gate", "up", "down")]
SPLIT_AT = {-5: [("kv", 0)], -4: [("kv", 1), ("kv", 2)], -3: [("kv", 3)], -2: [("q", 0)], -1: [("q", 1)],
            0: [("q", 2), ("o", 0)], 1: [("q", 3), ("o", 1)], 2: [("o", 2)], 3: [("o", 3)]}
ROUND_AT = dict(enumerate(range(len(FF_CHUNKS))))
RING = 4
CHUNK_COLS = 1024

FIRST_STEP, LAST_STEP = -6, STEPS + 6


def build(nc, x, ctx_in, g_xattn, g_ffn, wq, wk, wv, wo, wk_ctx, wv_ctx, q_norm_w, k_norm_w,
          gate_w, up_w, down_w, gate_scale, up_scale, down_scale, constants, out):
    f32, f32r, f16, bf16, u32 = (mybir.dt.float32, mybir.dt.float32r, mybir.dt.float16, mybir.dt.bfloat16,
                                 mybir.dt.uint32)
    ALU, ACT, AX = mybir.AluOpType, mybir.ActivationFunctionType, mybir.AxisListType

    with ExitStack() as stack:
        def sb(name, shape, dt=f32):
            return stack.enter_context(nc.sbuf_tensor(name, shape, dt))

        def bank(name):
            return stack.enter_context(nc.psum_tensor(name, [P, 512], f32))

        def sem(name):
            return stack.enter_context(nc.semaphore(name))

        const = sb("const", [P, C_ALL])
        mask = sb("mask", [P, LEN], bf16)
        ident_bf = sb("ident_bf", [P, P], bf16)
        ident = const[:, C_ID:C_ID + P]
        minus_half = sb("minus_half", [P, HPG])
        rope = sb("rope", [P, 4, DIM])
        k_w_col = sb("k_w_col", [P, 1])
        gates = sb("gates", [P, 2])
        tanh_gates = sb("tanh_gates", [P, 2])
        ff_rows = sb("ff_rows", [2 * FC, P])
        ff_scales = sb("ff_scales", [P, 2, FC])
        tanh_scale = sb("tanh_scale", [P, FC])
        fuse_scale = sb("fuse_scale", [P, FC])
        down_rows = sb("down_rows", [P, HID])

        x_sb = sb("x_sb", [P, TILES, HID])
        ctx_sb = sb("ctx_sb", [P, 2, HID])
        xn = sb("xn", [P, HID])
        stage = sb("stage", [P, RING, CHUNK_COLS])
        w_kv = [sb(f"w_kv_{a}", [P, 4, KC, GW], f32r) for a in ("hi", "lo")]
        w_q = [sb(f"w_q_{a}", [P, GROUPS, KC, GW], f32r) for a in ("hi", "lo")]
        w_o = [sb(f"w_o_{a}", [P, GROUPS, HPG, HID], f32r) for a in ("hi", "lo")]
        w_ff = sb("w_ff", [P, 2, KC, FF], f16)
        w_down = sb("w_down", [P, FC, HID], f32r)
        quant_m = sb("quant_m", [P, FF])

        xt = [sb(f"xt_{a}", [P, 2, 2 * KC, P], f32r) for a in ("hi", "lo")]
        kt = sb("kt", [P, 2, GROUPS, 4, LEN])
        v_hi = sb("v_hi", [P, 2, 2, GW], f32r)
        v_lo = sb("v_lo", [P, 2, 2, GW], f32r)
        q_rot = sb("q_rot", [P, HPG, DIM])
        q_sin = sb("q_sin", [P, HPG, DIM])
        qt = sb("qt", [P, 2, HPG, LEN])
        k_cos = sb("k_cos", [P, HPG, DIM])
        k_sin = sb("k_sin", [P, HPG, DIM])
        kn = k_sin
        probs = sb("probs", [P, 4, P])
        pt_hi = sb("pt_hi", [P, 512], f32r)
        pt_lo = sb("pt_lo", [P, 512], f32r)
        ot_hi = sb("ot_hi", [P, HPG, P], f32r)
        ot_lo = sb("ot_lo", [P, HPG, P], f32r)
        squares = const[:, 0:2 * DIM].bitcast(bf16).rearrange("p (h d) -> p h d", h=HPG)

        ssq = sb("ssq", [P, HPG])
        ssq_rows = sb("ssq_rows", [P, 4])
        q_scale = sb("q_scale", [P, 2, 4])
        row_max = sb("row_max", [P, 4])
        exp_bias = sb("exp_bias", [P, 4])
        row_sum = sb("row_sum", [P, 4])
        row_inv = sb("row_inv", [P, 4])
        k_ssq = sb("k_ssq", [P, HPG])
        k_var = sb("k_var", [P, HPG])
        k_inv = sb("k_inv", [P, HPG])
        ln_stats = sb("ln_stats", [P, 6])
        ln_mean = sb("ln_mean", [P, 2])
        ln_var = sb("ln_var", [P, 1])
        ln_inv = sb("ln_inv", [P, 1])
        x2_stats = sb("x2_stats", [P, 6])
        x2_mean = sb("x2_mean", [P, 2])
        x2_var = sb("x2_var", [P, 1])
        x2_inv = sb("x2_inv", [P, 1])

        x1 = sb("x1", [P, 2, HID])
        x2n = xn
        x2t = [sb(f"x2t_{a}", [P, KC, P], f16) for a in ("hi", "lo")]
        tanh_g = sb("tanh_g", [P, 2, P])
        fuse = sb("fuse", [P, 2, P])
        fuse_hi = sb("fuse_hi", [P, FC, P], f32r)
        fuse_lo = sb("fuse_lo", [P, FC, P], f32r)
        down_y = fuse[:, :, :].rearrange("p a n -> p (a n)")

        ps_t, ps_q, ps_s, ps_o, ps_f, ps_k, ps_y, ps_p = (
            bank(n) for n in ("ps_transposed", "ps_q", "ps_scores", "ps_attn", "ps_ff", "ps_kv", "ps_y", "ps_probs"))

        const_in, small_in, late_in, x0_in, x_in = (
            sem(n) for n in ("const_in", "small_in", "late_in", "x0_in", "x_in"))
        ctx_in_sem = [sem(f"ctx_in_{i}") for i in range(2)]
        chunk_in = [sem(f"chunk_in_{i}") for i in range(len(CHUNKS))]
        out_stored = [sem(f"out_stored_{i}") for i in range(2)]
        half_set = sem("half_set")
        tables_ready = sem("tables_ready")
        gates_ready = sem("gates_ready")
        scales_turned, scales_copied, scales_ready = sem("scales_turned"), sem("scales_copied"), sem("scales_ready")
        w_hi_ready, w_lo_ready = sem("w_hi_ready"), sem("w_lo_ready")
        wo_hi_ready, wo_lo_ready = sem("wo_hi_ready"), sem("wo_lo_ready")
        quant_exp, quant_round, quant_sum, quant_diff, quant_nan, quant_done = (
            sem(n) for n in ("quant_exp", "quant_round", "quant_sum", "quant_diff", "quant_nan", "quant_done"))
        ln_counted, ln_averaged, ln_var_ready, ln_inv_ready, xn_ready = (
            sem(n) for n in ("ln_counted", "ln_averaged", "ln_var_ready", "ln_inv_ready", "xn_ready"))
        xc_turned, xt_hi_ready, xt_lo_ready = sem("xc_turned"), sem("xt_hi_ready"), sem("xt_lo_ready")
        kv_made = {kind: sem(f"{kind}_made") for kind in KV_KINDS}
        kc_squared, kc_var_ready, kc_inv_ready, kc_ready, kc_turned, kc_stored = (
            sem(n) for n in ("kc_squared", "kc_var_ready", "kc_inv_ready", "kc_ready", "kc_turned", "kc_stored"))
        ks_squared, ks_var_ready, ks_inv_ready, ks_roped, ks_added, ks_ready, ks_turned, ks_stored = (
            sem(n) for n in ("ks_squared", "ks_var_ready", "ks_inv_ready", "ks_roped", "ks_added", "ks_ready",
                             "ks_turned", "ks_stored"))
        vc_hi_ready, vc_lo_ready, vs_hi_ready, vs_lo_ready = (
            sem(n) for n in ("vc_hi_ready", "vc_lo_ready", "vs_hi_ready", "vs_lo_ready"))
        x1_ready, x2_counted, x2_averaged, x2_var_ready, x2_inv_ready, x2_ready, x2_turned, x2_hi_ready, x2_lo_ready = (
            sem(n) for n in ("x1_ready", "x2_counted", "x2_averaged", "x2_var_ready", "x2_inv_ready", "x2_ready",
                             "x2_turned", "x2_hi_ready", "x2_lo_ready"))
        ff_made, tanh_ready, gated_ready, fuse_ready, fuse_hi_ready, fuse_lo_ready = (
            sem(n) for n in ("ff_made", "tanh_ready", "gated_ready", "fuse_ready", "fuse_hi_ready", "fuse_lo_ready"))
        down_made, down_scaled, result_ready = sem("down_made"), sem("down_scaled"), sem("result_ready")
        q_made, q_squared, q_cos_ready, q_sin_ready, q_rot_ready, ssq_moved, q_scale_ready, q_turned, qt_ready = (
            sem(n) for n in ("q_made", "q_squared", "q_cos_ready", "q_sin_ready", "q_rot_ready", "ssq_moved",
                             "q_scale_ready", "q_turned", "qt_ready"))
        scores_made, max_ready, bias_ready, exp_ready, inv_ready, probs_ready, probs_turned, pt_hi_ready, pt_lo_ready = (
            sem(n) for n in ("scores_made", "max_ready", "bias_ready", "exp_ready", "inv_ready", "probs_ready",
                             "probs_turned", "pt_hi_ready", "pt_lo_ready"))
        attn_made, ot_hi_ready, ot_lo_ready, y_made = (
            sem(n) for n in ("attn_made", "ot_hi_ready", "ot_lo_ready", "y_made"))

        def step(u, k):
            return u * (2 * GROUPS) + k

        def tile(u, m):
            return u * 2 + m

        def is_step(u, k):
            return not isinstance(u, int) or 0 <= step(u, k) < STEPS

        def is_tile(u, m):
            return not isinstance(u, int) or 0 <= tile(u, m) < TILES

        def run_steps(eng, one_step):
            for k in range(FIRST_STEP, 2 * GROUPS):
                one_step(0, k)
            with eng.Fori(1, TILES // 2 - 1) as u:
                for k in range(2 * GROUPS):
                    one_step(u, k)
            last = TILES // 2 - 1
            for k in range(LAST_STEP - step(last, 0)):
                one_step(last, k)

        def at_step(u, k):
            return step(u, k) if isinstance(u, int) else None

        def kv_bank(u, m, j):
            return (ps_k, ps_f, ps_o, ps_p)[j] if first_tile(u, m) else ps_k

        def ff_bank(u, m, piece):
            return {0: ps_f, 1: ps_k, 2: ps_s, None: ps_q}[piece] if last_tile(u, m) else ps_f

        def first_tile(u, m):
            return isinstance(u, int) and tile(u, m) == 0

        def last_tile(u, m):
            return isinstance(u, int) and tile(u, m) == TILES - 1

        def four(ap):
            return ap[:, :].rearrange("p (h d) -> p h d", h=4)

        def rotated(ap):
            return ap.rearrange("p h (f j) -> p h f j", f=2)[:, :, ::-1, :]

        def halves(ap):
            return ap.rearrange("p h (f j) -> p h f j", f=2)

        def over_heads(row):
            return row.unsqueeze(1).broadcast_to([P, HPG, DIM])

        def staged(n, cols):
            return stage[:, n % RING, 0:cols]

        block = stack.enter_context(nc.Block())

        @block.sync
        def _(sp):
            x_by_half = x.rearrange("(t c) l n -> c l t n", c=2)
            out_by_half = out.rearrange("(t c) l n -> c l t n", c=2)
            ctx_rows = ctx_in.rearrange("(t c) l n -> (c l) t n", c=2)
            kv_views = [w.rearrange("(c p) n -> p c n", p=P) for w in (wk_ctx, wk, wv_ctx, wv)]
            wq_view = wq.rearrange("(c p) (g n) -> p g c n", p=P, g=GROUPS)
            wo_view = wo.rearrange("(g h p) n -> p g h n", p=P, g=GROUPS)
            ff_views = {"gate": gate_w, "up": up_w}
            down_view = down_w.rearrange("(c p) n -> p c n", p=P)

            def load_chunk(n):
                kind, i = CHUNKS[n]
                if n >= RING:
                    before = n - RING
                    kind_before, i_before = CHUNKS[before]
                    if kind_before == "o":
                        sp.wait_ge(wo_lo_ready, i_before + 1)
                    elif kind_before in ("kv", "q"):
                        sp.wait_ge(w_lo_ready, i_before + (kind_before == "q") * len(KV_KINDS) + 1)
                    else:
                        sp.wait_ge(quant_done, FF_CHUNKS.index(CHUNKS[before]) + 1)
                if kind == "kv":
                    sp.dma_start(staged(n, CHUNK_COLS).rearrange("p (c n) -> p c n", c=KC), kv_views[i])\
                      .then_inc(chunk_in[n], 16)
                elif kind == "q":
                    sp.dma_start(staged(n, CHUNK_COLS).rearrange("p (c n) -> p c n", c=KC), wq_view[:, i])\
                      .then_inc(chunk_in[n], 16)
                elif kind == "o":
                    sp.dma_start(staged(n, CHUNK_COLS).rearrange("p (h n) -> p h n", h=HPG), wo_view[:, i])\
                      .then_inc(chunk_in[n], 16)
                elif kind == "down":
                    sp.dma_start(staged(n, FF).rearrange("p (c n) -> p c n", c=FC // 2),
                                 down_view[:, i * (FC // 2):(i + 1) * (FC // 2), :]).then_inc(chunk_in[n], 16)
                else:
                    sp.dma_start(staged(n, FF), ff_views[kind][i * P:(i + 1) * P, :]).then_inc(chunk_in[n], 16)

            for r in range(2):
                sp.dma_start(x_sb[r * LEN:(r + 1) * LEN, 0, :], x_by_half[1 - r][:, 0, :]).then_inc(x0_in, 16)
            sp.dma_start(ctx_sb[:, 0, :], ctx_rows[:, 0, :]).then_inc(ctx_in_sem[0], 16)
            sp.dma_start(const[:, :], constants).then_inc(const_in, 16)
            load_chunk(0)
            load_chunk(1)
            for n, w in enumerate((q_norm_w, k_norm_w)):
                row = w.rearrange("(a d) -> a d", a=1)
                sp.dma_start(rope[:, 2 * n, :], row.broadcast_to([P, DIM])).then_inc(small_in, 16)
                for f in range(2):
                    sp.dma_start(rope[:, 2 * n + 1, f * HALF:(f + 1) * HALF],
                                 row[:, (1 - f) * HALF:(2 - f) * HALF].broadcast_to([P, HALF])).then_inc(small_in, 16)
            sp.dma_start(k_w_col[:, :], k_norm_w.rearrange("(d a) -> d a", a=1)).then_inc(small_in, 16)
            for n in range(2, RING):
                load_chunk(n)
            for n, w in enumerate((g_xattn, g_ffn)):
                sp.dma_start(gates[:, n:n + 1], w.rearrange("(a n) -> a n", a=1).broadcast_to([P, 1]))\
                  .then_inc(late_in, 16)
            for n, w in enumerate((gate_scale, up_scale)):
                sp.dma_start(ff_rows[n * FC:(n + 1) * FC, :], w.rearrange("(c p) -> c p", p=P)).then_inc(late_in, 16)
            sp.dma_start(down_rows[:, :], down_scale.rearrange("(a n) -> a n", a=1).broadcast_to([P, HID]))\
              .then_inc(late_in, 16)
            sp.dma_start(ctx_sb[:, 1, :], ctx_rows[:, 1, :]).then_inc(ctx_in_sem[1], 16)
            for r in range(2):
                sp.dma_start(x_sb[r * LEN:(r + 1) * LEN, 1:TILES, :], x_by_half[1 - r][:, 1:TILES, :])\
                  .then_inc(x_in, 16)
            for n in range(RING, len(CHUNKS)):
                load_chunk(n)

            def store_tile(u, m):
                sp.wait_ge(result_ready, tile(u, m) + 1)
                for r in range(2):
                    sp.dma_start(out_by_half[1 - r][:, bass.ds(tile(u, m), 1), :],
                                 x1[r * LEN:(r + 1) * LEN, m % 2, :].unsqueeze(1)).then_inc(out_stored[m % 2], 16)

            def pair(u):
                for m in range(2):
                    if is_tile(u, m + 2):
                        sp.wait_ge(xc_turned, tile(u, m) + 1)
                        sp.dma_start(ctx_sb[:, m, :].unsqueeze(1), ctx_rows[:, bass.ds(tile(u, m + 2), 1), :])\
                          .then_inc(ctx_in_sem[m], 16)
                for m in range(2):
                    if is_tile(u, m - 2):
                        store_tile(u, m - 2)

            pair(0)
            with sp.Fori(1, TILES // 2 - 1) as u:
                pair(u)
            pair(TILES // 2 - 1)
            pair(TILES // 2)
            for m in range(2):
                sp.wait_ge(out_stored[m], 16 * 2 * (TILES // 2))

        @block.tensor
        def _(pe):
            def three_passes(dst, lhs, rhs, terms):
                n, passes = 0, [(0, 0), (0, 1), (1, 0)]
                for i in range(terms):
                    for a, b in passes:
                        last = nc.tensor.matmul(dst, lhs(a, i), rhs(b, i), start=(n == 0),
                                                stop=(n == 3 * terms - 1))
                        n += 1
                return last

            def turn(dst, srcs):
                for i, src in enumerate(srcs):
                    last = nc.tensor.matmul(dst[:, i * P:(i + 1) * P], src, ident, start=True, stop=True,
                                            is_transpose=True)
                return last

            def one_step(u, k):
                m, j = divmod(k, GROUPS)
                par, nxt = m % 2, (m + 1) % 2

                if is_step(u, k):
                    pe.wait_ge(q_rot_ready, step(u, k) + 1)
                    if j == 1 and is_tile(u, m + 1):
                        pe.wait_ge(xt_lo_ready, tile(u, m + 1) + 1)
                    if j == 2 and is_tile(u, m + 1):
                        pe.wait_ge(kc_stored, tile(u, m + 1) + 1)
                    if j == 3 and is_tile(u, m - 1):
                        pe.wait_ge(x2_lo_ready, tile(u, m - 1) + 1)
                    if j == 0:
                        pe.wait_ge(ks_stored, tile(u, m) + 1)
                    turn(ps_t, [q_rot[:, h, :] for h in range(HPG)]).then_inc(q_turned, 1)

                if is_step(u, k + 1):
                    g1 = (k + 1) % GROUPS
                    p1 = ((k + 1) // GROUPS) % 2
                    if isinstance(u, int) and 0 <= step(u, k + 1) < GROUPS:
                        pe.wait_ge(w_lo_ready, len(KV_KINDS) + step(u, k + 1) + 1)
                        pe.wait_ge(w_hi_ready, len(KV_KINDS) + step(u, k + 1) + 1)
                    pe.wait_ge(xt_lo_ready, tile(u, (k + 1) // GROUPS) + 1)
                    if is_step(u, k):
                        pe.wait_ge(q_squared, step(u, k) + 1)
                    three_passes(ps_q[:, :], lambda a, i: xt[a][:, p1, i, :], lambda b, i: w_q[b][:, g1, i, :], KC)\
                        .then_inc(q_made, 1)

                if is_step(u, k):
                    pe.wait_ge(qt_ready, step(u, k) + 1)
                if j == 0 and is_tile(u, m + 1):
                    pe.wait_ge(xn_ready, tile(u, m + 1) + 1)
                    if isinstance(u, int) and tile(u, m + 1) == 0:
                        pe.wait_ge(const_in, 16)
                    pe.wait_ge(ctx_in_sem[nxt], 16 * (u + (m + 1) // 2 + 1))
                    turn(ps_t, [xn[:, i * P:(i + 1) * P] for i in range(KC)]
                         + [ctx_sb[:, nxt, i * P:(i + 1) * P] for i in range(KC)]).then_inc(xc_turned, 1)
                if j == 2 and is_tile(u, m - 1):
                    pe.wait_ge(x2_ready, tile(u, m - 1) + 1)
                    turn(ps_t, [x2n[:, i * P:(i + 1) * P] for i in range(KC)]).then_inc(x2_turned, 1)
                if j == 3 and is_tile(u, m + 1):
                    pe.wait_ge(ks_ready, tile(u, m + 1) + 1)
                    turn(ps_t, [kn[:, h, :] for h in range(GROUPS)]).then_inc(ks_turned, 1)

                if is_step(u, k):
                    if j == 0:
                        pe.wait_ge(ks_stored, tile(u, m) + 1)
                    if isinstance(u, int) and step(u, k) == 0:
                        pe.wait_ge(tables_ready, 6)
                    scores = four(ps_s)
                    for r in range(2):
                        nc.tensor.matmul(scores[:, 2 * r:2 * r + 2, r * LEN:(r + 1) * LEN], ident_bf[:, :],
                                         mask[:, :].unsqueeze(1).broadcast_to([P, 2, LEN]),
                                         start=(r == 0), stop=False, skip_group_check=True)
                    for r in range(2):
                        for pp in range(2):
                            last = nc.tensor.matmul(scores[:, 2 * r + pp, :],
                                                    qt[:, r, 2 * pp:2 * pp + 2, :],
                                                    kt[:, par, j, 2 * r:2 * r + 2, :],
                                                    start=False, stop=(r == 1 and pp == 1), skip_group_check=True)
                    last.then_inc(scores_made, 1)

                if is_step(u, k - 1):
                    g0, p0 = (k - 1) % GROUPS, ((k - 1) // GROUPS) % 2
                    pe.wait_ge(pt_lo_ready, step(u, k - 1) + 1)
                    if g0 == 0:
                        pe.wait_ge(vs_lo_ready, tile(u, (k - 1) // GROUPS) + 1)
                    for r in range(2):
                        v = (v_hi, v_lo)
                        pt = (pt_hi, pt_lo)
                        last = three_passes(ps_o[:, r * 256:(r + 1) * 256],
                                            lambda a, i: v[a][:, p0, r, g0 * DIM:(g0 + 1) * DIM],
                                            lambda b, i: pt[b][:, r * 256:(r + 1) * 256], 1)
                    last.then_inc(attn_made, 1)

                if at_step(u, k) == -2:
                    pe.wait_ge(late_in, 16 * 5)
                    nc.tensor.matmul(ps_y[:, 0:2 * FC], ff_rows[:, :], ident[0:2 * FC, 0:2 * FC], start=True, stop=True,
                                     is_transpose=True).then_inc(scales_turned, 1)

                piece, ff_m = {2: (0, m - 1), 3: (1, m - 1), 0: (2, m - 2), 1: (None, m - 2)}[j]
                if is_tile(u, ff_m) and piece is not None:
                    pe.wait_ge(x2_lo_ready, tile(u, ff_m) + 1)
                    if isinstance(u, int) and tile(u, ff_m) == 0:
                        pe.wait_ge(quant_done, 4)
                    if piece == 0 and is_tile(u, ff_m - 1):
                        pe.wait_ge(down_scaled, tile(u, ff_m))
                    elif piece > 0 and not last_tile(u, ff_m):
                        pe.wait_ge(fuse_ready, tile(u, ff_m) * 3 + piece)
                    bank_f = ff_bank(u, ff_m, piece)
                    for i, (w, c) in enumerate(((0, 2 * piece), (0, 2 * piece + 1), (1, 2 * piece), (1, 2 * piece + 1))):
                        n = 0
                        for kc in range(KC):
                            for a in range(2):
                                last = nc.tensor.matmul(bank_f[:, i * P:(i + 1) * P],
                                                        w_ff[:, w, kc, c * P:(c + 1) * P], x2t[a][:, kc, :],
                                                        start=(n == 0), stop=(n == 2 * KC - 1))
                                n += 1
                    last.then_inc(ff_made, 1)
                if is_tile(u, ff_m) and piece is None:
                    if isinstance(u, int) and tile(u, ff_m) == 0:
                        pe.wait_ge(quant_done, 6)
                    pe.wait_ge(fuse_ready, tile(u, ff_m) * 3 + 3)
                    pe.wait_ge(fuse_lo_ready, tile(u, ff_m) * 3 + 3)
                    for c in range(FC):
                        for a, part in enumerate((fuse_hi, fuse_lo)):
                            last = nc.tensor.matmul(ff_bank(u, ff_m, piece)[:, 0:HID], part[:, c, :], w_down[:, c, :],
                                                    start=(c == 0 and a == 0), stop=(c == FC - 1 and a == 1))
                    last.then_inc(down_made, 1)

                if is_tile(u, m + 1):
                    kind = KV_KINDS[j]
                    t1 = tile(u, m + 1)
                    pe.wait_ge(xt_lo_ready, t1 + 1)
                    if isinstance(u, int) and t1 == 0:
                        pe.wait_ge(w_hi_ready, j + 1)
                        pe.wait_ge(w_lo_ready, j + 1)
                    if j == 0 and is_tile(u, m):
                        pe.wait_ge(vs_lo_ready, t1)
                    if j == 1 and not first_tile(u, m + 1):
                        pe.wait_ge(kc_ready, t1 + 1)
                    if j == 2 and not first_tile(u, m + 1):
                        pe.wait_ge(ks_roped, t1 + 1)
                    if j == 3 and not first_tile(u, m + 1):
                        pe.wait_ge(vc_lo_ready, t1 + 1)
                    base = KC if kind.endswith("ctx") else 0
                    three_passes(kv_bank(u, m + 1, j)[:, :], lambda a, i: xt[a][:, nxt, base + i, :], lambda b, i: w_kv[b][:, j, i, :],
                                 KC).then_inc(kv_made[kind], 1)

                if j == 1 and is_tile(u, m + 1):
                    pe.wait_ge(kc_ready, tile(u, m + 1) + 1)
                    turn(ps_t, [kn[:, h, :] for h in range(GROUPS)]).then_inc(kc_turned, 1)

                if is_step(u, k - 1):
                    g0 = (k - 1) % GROUPS
                    m0 = (k - 1) // GROUPS
                    pe.wait_ge(ot_lo_ready, step(u, k - 1) + 1)
                    if isinstance(u, int) and 0 <= step(u, k - 1) < GROUPS:
                        pe.wait_ge(wo_lo_ready, g0 + 1)
                    if g0 == 0 and is_tile(u, m0 - 1):
                        pe.wait_ge(x1_ready, tile(u, m0))
                    ot = (ot_hi, ot_lo)
                    n = 0
                    for h in range(HPG):
                        for a, b in ((0, 0), (0, 1), (1, 0)):
                            last = nc.tensor.matmul(ps_y[:, 0:HID], ot[a][:, h, :], w_o[b][:, g0, h, :],
                                                    start=(g0 == 0 and n == 0),
                                                    stop=(g0 == GROUPS - 1 and n == 3 * HPG - 1))
                            n += 1
                    last.then_inc(y_made, 1)

                if is_step(u, k):
                    pe.wait_ge(probs_ready, step(u, k) + 1)
                    turn(ps_p, [probs[:, i, :] for i in range(4)]).then_inc(probs_turned, 1)

            run_steps(pe, one_step)

        @block.scalar
        def _(act):
            def weight_hi(kind, i):
                n = CHUNKS.index((kind, i))
                act.wait_ge(chunk_in[n], 16)
                dst = {"kv": w_kv, "q": w_q, "o": w_o}[kind][0]
                nc.scalar.activation(dst[:, i].rearrange("p c n -> p (c n)"), staged(n, CHUNK_COLS), ACT.Copy)\
                    .then_inc(wo_hi_ready if kind == "o" else w_hi_ready, 1)

            def square_heads(src, dst):
                for h in range(HPG):
                    last = nc.scalar.activation(squares[:, h, :], src[:, h * DIM:(h + 1) * DIM], ACT.Square,
                                                accum_out=dst[:, h:h + 1])
                return last

            def one_step(u, k):
                m, j = divmod(k, GROUPS)
                par, nxt = m % 2, (m + 1) % 2

                if is_step(u, k):
                    act.wait_ge(q_turned, step(u, k) + 1)
                    nc.scalar.activation(qt[:, :, :, :], ps_t[:, :].rearrange("p (h r l) -> p r h l", h=HPG, r=2),
                                         ACT.Copy).then_inc(qt_ready, 1)

                if j == 0 and is_tile(u, m + 1):
                    act.wait_ge(xc_turned, tile(u, m + 1) + 1)
                    nc.scalar.activation(xt[0][:, nxt, :, :], four(ps_t), ACT.Copy).then_inc(xt_hi_ready, 1)
                if j == 2 and is_tile(u, m - 1):
                    act.wait_ge(x2_turned, tile(u, m - 1) + 1)
                    nc.scalar.activation(x2t[0][:, :, :].rearrange("p c n -> p (c n)"), ps_t[:, 0:HID], ACT.Copy)\
                        .then_inc(x2_hi_ready, 1)
                if j == 3 and is_tile(u, m + 1):
                    act.wait_ge(ks_turned, tile(u, m + 1) + 1)
                    nc.scalar.activation(kt[:, nxt, :, 0:4:3, :],
                                         ps_t[:, :].rearrange("p (g c m) -> p g c m", g=GROUPS, c=2), ACT.Copy)\
                        .then_inc(ks_stored, 1)

                if is_step(u, k + 1):
                    act.wait_ge(q_sin_ready, step(u, k + 1) + 1)
                    if is_step(u, k):
                        act.wait_ge(ssq_moved, step(u, k) + 1)
                    if j == 1 and is_tile(u, m + 1):
                        act.wait_ge(kc_squared, tile(u, m + 1) + 1)
                    if j == 2 and is_tile(u, m + 1):
                        act.wait_ge(ks_squared, tile(u, m + 1) + 1)
                    square_heads(ps_q, ssq).then_inc(q_squared, 1)

                if is_step(u, k - 1):
                    act.wait_ge(attn_made, step(u, k - 1) + 1)
                    nc.scalar.activation(ot_hi[:, :, :].rearrange("p h (r l) -> p r h l", r=2),
                                         ps_o[:, :].rearrange("p (r h l) -> p r h l", r=2, h=HPG), ACT.Copy)\
                        .then_inc(ot_hi_ready, 1)

                if is_step(u, k):
                    act.wait_ge(bias_ready, step(u, k) + 1)
                    for i in range(4):
                        last = nc.scalar.activation(probs[:, i, :], ps_s[:, i * P:(i + 1) * P], ACT.Exp,
                                                    bias=exp_bias[:, i:i + 1], scale=q_scale[:, k % 2, i:i + 1],
                                                    accum_out=row_sum[:, i:i + 1])
                    last.then_inc(exp_ready, 1)

                piece, ff_m = {2: (0, m - 1), 3: (1, m - 1), 0: (2, m - 2), 1: (None, m - 2)}[j]
                if is_tile(u, ff_m) and piece is not None:
                    act.wait_ge(ff_made, tile(u, ff_m) * 3 + piece + 1)
                    if isinstance(u, int) and tile(u, ff_m) == 0 and piece == 0:
                        act.wait_ge(scales_ready, 2)
                    if piece > 0 and last_tile(u, ff_m):
                        act.wait_ge(fuse_ready, tile(u, ff_m) * 3 + piece)
                    for i in range(2):
                        c = 2 * piece + i
                        last = nc.scalar.activation(tanh_g[:, i, :], ff_bank(u, ff_m, piece)[:, i * P:(i + 1) * P], ACT.Tanh,
                                                    scale=tanh_scale[:, c:c + 1])
                    last.then_inc(tanh_ready, 1)

                for kind, i in SPLIT_AT.get(at_step(u, k), ()):
                    weight_hi(kind, i)

                if is_tile(u, m + 1):
                    t1 = tile(u, m + 1)
                    act.wait_ge(kv_made[KV_KINDS[j]], t1 + 1)
                    if j in (0, 1) and is_step(u, k + 1):
                        act.wait_ge(q_squared, step(u, k + 1) + 1)
                    if j == 0:
                        if isinstance(u, int) and t1 == 0:
                            act.wait_ge(tables_ready, 6)
                        if is_tile(u, m):
                            act.wait_ge(ks_var_ready, t1)
                        square_heads(kv_bank(u, m + 1, j), k_ssq).then_inc(kc_squared, 1)
                    if j == 1:
                        act.wait_ge(kc_var_ready, t1 + 1)
                        square_heads(kv_bank(u, m + 1, j), k_ssq).then_inc(ks_squared, 1)
                    if j == 2:
                        for c in range(2):
                            last = nc.scalar.activation(v_hi[c * LEN:(c + 1) * LEN, nxt, 1 - c, :],
                                                        kv_bank(u, m + 1, j)[c * LEN:(c + 1) * LEN, :], ACT.Copy)
                        last.then_inc(vc_hi_ready, 1)
                    if j == 3:
                        for r in range(2):
                            last = nc.scalar.activation(v_hi[r * LEN:(r + 1) * LEN, nxt, r, :],
                                                        kv_bank(u, m + 1, j)[r * LEN:(r + 1) * LEN, :], ACT.Copy)
                        last.then_inc(vs_hi_ready, 1)

                if j == 1 and is_tile(u, m + 1):
                    act.wait_ge(kc_turned, tile(u, m + 1) + 1)
                    nc.scalar.activation(kt[:, nxt, :, 2:0:-1, :],
                                         ps_t[:, :].rearrange("p (g c m) -> p g c m", g=GROUPS, c=2), ACT.Copy,
                                         scale=k_w_col[:, 0:1]).then_inc(kc_stored, 1)

                if is_tile(u, ff_m) and piece is not None:
                    act.wait_ge(fuse_ready, tile(u, ff_m) * 3 + piece + 1)
                    nc.scalar.activation(fuse_hi[:, 2 * piece:2 * piece + 2, :], fuse[:, :, :], ACT.Copy)\
                        .then_inc(fuse_hi_ready, 1)

                if at_step(u, k) == -1:
                    act.wait_ge(late_in, 16 * 5)
                    nc.scalar.activation(tanh_gates[:, :], gates[:, :], ACT.Tanh).then_inc(gates_ready, 1)

                if is_step(u, k):
                    act.wait_ge(probs_turned, step(u, k) + 1)
                    nc.scalar.activation(pt_hi[:, :], ps_p[:, :], ACT.Copy).then_inc(pt_hi_ready, 1)

            run_steps(act, one_step)

        @block.vector
        def _(dve):
            def as_f32(ap):
                return ap.bitcast(f32)

            def weight_lo(kind, i):
                n = CHUNKS.index((kind, i))
                dve.wait_ge(w_hi_ready, i + (kind == "q") * len(KV_KINDS) + 1)
                hi, lo = {"kv": w_kv, "q": w_q}[kind]
                nc.vector.tensor_tensor(lo[:, i].rearrange("p c n -> p (c n)"), staged(n, CHUNK_COLS),
                                        as_f32(hi[:, i].rearrange("p c n -> p (c n)")), ALU.subtract)\
                    .then_inc(w_lo_ready, 1)

            def rounding_constant(i):
                n = CHUNKS.index(FF_CHUNKS[i])
                dve.wait_ge(chunk_in[n], 16)
                if i:
                    dve.wait_ge(quant_done, i)
                nc.vector.tensor_scalar(quant_m[:, :].bitcast(u32), staged(n, FF).bitcast(u32), EXPONENT_BITS, None,
                                        ALU.bitwise_and).then_inc(quant_exp, 1)
                dve.wait_ge(quant_exp, i + 1)
                nc.vector.tensor_scalar(quant_m[:, :], quant_m[:, :], E4M3_MIN_NORMAL, E4M3_ROUNDER,
                                        ALU.max, ALU.mult).then_inc(quant_round, 1)

            def round_weights(i):
                n = CHUNKS.index(FF_CHUNKS[i])
                dve.wait_ge(quant_round, i + 1)
                nc.vector.tensor_tensor(staged(n, FF), staged(n, FF), quant_m[:, :], ALU.add).then_inc(quant_sum, 1)
                dve.wait_ge(quant_sum, i + 1)
                nc.vector.tensor_tensor(staged(n, FF), staged(n, FF), quant_m[:, :], ALU.subtract)\
                    .then_inc(quant_diff, 1)

            def out_of_range(i):
                n = CHUNKS.index(FF_CHUNKS[i])
                dve.wait_ge(quant_diff, i + 1)
                nc.vector.tensor_scalar(quant_m[:, :], staged(n, FF), E4M3_OVERFLOW, 0.0, ALU.mult, ALU.mult)\
                    .then_inc(quant_nan, 1)

            def tables():
                dve.wait_ge(const_in, 16)
                nc.vector.tensor_copy(mask[:, :], const[:, C_MASK:C_MASK + LEN]).then_inc(tables_ready, 1)
                nc.vector.tensor_copy(ident_bf[:, :], ident).then_inc(tables_ready, 1)
                dve.wait_ge(small_in, 16 * 7)
                for n in range(4):
                    col = C_COS if n % 2 == 0 else C_SIN
                    nc.vector.tensor_tensor(rope[:, n, :], const[:, col:col + DIM], rope[:, n, :], ALU.mult)\
                        .then_inc(tables_ready, 1)
            def scales():
                dve.wait_ge(scales_turned, 1)
                nc.vector.tensor_copy(ff_scales[:, :, :].rearrange("p a c -> p (a c)"), ps_y[:, 0:2 * FC])\
                    .then_inc(scales_copied, 1)
                dve.wait_ge(scales_copied, 1)
                nc.vector.tensor_scalar(tanh_scale[:, :], ff_scales[:, 0, :], 0.5 / FF_IN_SCALE, None, ALU.mult)\
                    .then_inc(scales_ready, 1)
                nc.vector.scalar_tensor_tensor(fuse_scale[:, :], ff_scales[:, 0, :], 0.5 / FF_IN_SCALE ** 2,
                                               ff_scales[:, 1, :], ALU.mult, ALU.mult).then_inc(scales_ready, 1)

            def down_row_scale():
                dve.wait_ge(gates_ready, 1)
                nc.vector.tensor_scalar(down_rows[:, :], down_rows[:, :], tanh_gates[:, 1:2], None, ALU.mult)\
                    .then_inc(scales_ready, 1)

            def x_tile(u, m):
                if isinstance(u, int):
                    return x_sb[:, tile(u, m), :]
                return x_sb[:, bass.ds(tile(u, m), 1), :].rearrange("p a n -> p (a n)")

            def one_step(u, k):
                m, j = divmod(k, GROUPS)
                par, nxt = m % 2, (m + 1) % 2

                if j == 3 and is_tile(u, m + 2):
                    dve.wait_ge(ln_inv_ready, tile(u, m + 2) + 1)
                    if is_tile(u, m + 1):
                        dve.wait_ge(xc_turned, tile(u, m + 1) + 1)
                    if is_tile(u, m - 1):
                        dve.wait_ge(x2_turned, tile(u, m - 1) + 1)
                    nc.vector.tensor_scalar(xn[:, :], x_tile(u, m + 2), ln_mean[:, 0:1], ln_inv[:, 0:1],
                                            ALU.subtract, ALU.mult).then_inc(xn_ready, 1)

                if is_step(u, k + 1):
                    dve.wait_ge(q_made, step(u, k + 1) + 1)
                    if is_step(u, k):
                        dve.wait_ge(q_turned, step(u, k) + 1)
                    nc.vector.tensor_tensor(q_rot[:, :, :], four(ps_q), over_heads(rope[:, 0, :]), ALU.mult)\
                        .then_inc(q_cos_ready, 1)
                if j == 2 and is_tile(u, m - 1):
                    dve.wait_ge(x2_hi_ready, tile(u, m - 1) + 1)
                    nc.vector.tensor_tensor(x2t[1][:, :, :].rearrange("p c n -> p (c n)"), ps_t[:, 0:HID],
                                            x2t[0][:, :, :].rearrange("p c n -> p (c n)"), ALU.subtract)\
                        .then_inc(x2_lo_ready, 1)
                if is_step(u, k + 1):
                    if is_step(u, k):
                        dve.wait_ge(q_rot_ready, step(u, k) + 1)
                    nc.vector.tensor_tensor(halves(q_sin[:, :, :]), rotated(four(ps_q)), halves(over_heads(rope[:, 1, :])),
                                            ALU.mult).then_inc(q_sin_ready, 1)

                if is_step(u, k):
                    dve.wait_ge(scores_made, step(u, k) + 1)
                    nc.vector.tensor_reduce(row_max[:, :], four(ps_s), AX.X, ALU.max).then_inc(max_ready, 1)
                    dve.wait_ge(max_ready, step(u, k) + 1)
                    dve.wait_ge(q_scale_ready, step(u, k) + 1)
                    nc.vector.scalar_tensor_tensor(exp_bias[:, :], row_max[:, :], -1.0, q_scale[:, k % 2, :],
                                                   ALU.mult, ALU.mult).then_inc(bias_ready, 1)

                if j == 1 and is_tile(u, m + 1):
                    dve.wait_ge(kc_inv_ready, tile(u, m + 1) + 1)
                    if is_tile(u, m):
                        dve.wait_ge(ks_turned, tile(u, m) + 1)
                    nc.vector.tensor_tensor(kn[:, :, :], four(kv_bank(u, m + 1, 0)), k_inv[:, :].unsqueeze(2).broadcast_to([P, HPG, DIM]),
                                            ALU.mult).then_inc(kc_ready, 1)
                if j == 0 and is_tile(u, m + 1):
                    dve.wait_ge(xt_hi_ready, tile(u, m + 1) + 1)
                    nc.vector.tensor_tensor(xt[1][:, nxt, :, :], four(ps_t), as_f32(xt[0][:, nxt, :, :]), ALU.subtract)\
                        .then_inc(xt_lo_ready, 1)
                if is_step(u, k + 1):
                    dve.wait_ge(q_squared, step(u, k + 1) + 1)
                    if is_step(u, k):
                        dve.wait_ge(q_scale_ready, step(u, k) + 1)
                    for r in range(2):
                        for hh in range(2):
                            last = nc.vector.tensor_scalar(ssq_rows[hh * LEN:(hh + 1) * LEN, 2 * r:2 * r + 2],
                                                           ssq[r * LEN:(r + 1) * LEN, hh::2], DIM * RMS_EPS, None,
                                                           ALU.add)
                    last.then_inc(ssq_moved, 1)

                if is_step(u, k - 1):
                    dve.wait_ge(ot_hi_ready, step(u, k - 1) + 1)
                    nc.vector.tensor_tensor(ot_lo[:, :, :].rearrange("p h (r l) -> p r h l", r=2),
                                            ps_o[:, :].rearrange("p (r h l) -> p r h l", r=2, h=HPG),
                                            as_f32(ot_hi[:, :, :]).rearrange("p h (r l) -> p r h l", r=2), ALU.subtract)\
                        .then_inc(ot_lo_ready, 1)

                if at_step(u, k) in ROUND_AT:
                    rounding_constant(ROUND_AT[step(u, k)])

                ln_now = j == 2 and is_tile(u, m + 2)
                ln_count = tile(u, m + 2) + 1
                if ln_now:
                    if isinstance(u, int) and tile(u, m + 2) == 0:
                        dve.wait_ge(x0_in, 32)
                    if isinstance(u, int) and tile(u, m + 2) == 1:
                        dve.wait_ge(x_in, 32)
                    nc.vector.bn_stats(ln_stats[:, :], x_tile(u, m + 2)).then_inc(ln_counted, 1)
                    dve.wait_ge(ln_counted, ln_count)

                if is_step(u, k):
                    dve.wait_ge(exp_ready, step(u, k) + 1)
                    nc.vector.reciprocal(row_inv[:, :], row_sum[:, :]).then_inc(inv_ready, 1)

                if ln_now:
                    nc.vector.bn_aggr(ln_mean[:, :], ln_stats[:, :]).then_inc(ln_averaged, 1)
                    dve.wait_ge(ln_averaged, ln_count)
                    if is_tile(u, m + 1):
                        dve.wait_ge(ln_inv_ready, ln_count - 1)
                    nc.vector.tensor_scalar(ln_var[:, :], ln_mean[:, 1:2], LN_EPS, None, ALU.add).then_inc(ln_var_ready, 1)

                piece, ff_m = {2: (0, m - 1), 3: (1, m - 1), 0: (2, m - 2), 1: (None, m - 2)}[j]
                if is_tile(u, ff_m) and piece is not None:
                    count = tile(u, ff_m) * 3 + piece + 1
                    dve.wait_ge(tanh_ready, count)
                    nc.vector.scalar_tensor_tensor(tanh_g[:, :, :].rearrange("p a n -> p (a n)"),
                                                   tanh_g[:, :, :].rearrange("p a n -> p (a n)"), 1.0,
                                                   ff_bank(u, ff_m, piece)[:, 0:2 * P], ALU.add, ALU.mult).then_inc(gated_ready, 1)
                    dve.wait_ge(gated_ready, count)
                    if piece > 0:
                        dve.wait_ge(fuse_lo_ready, count - 1)
                    elif is_tile(u, ff_m - 1):
                        dve.wait_ge(result_ready, tile(u, ff_m))
                    for i in range(2):
                        c = 2 * piece + i
                        last = nc.vector.scalar_tensor_tensor(fuse[:, i, :], tanh_g[:, i, :], fuse_scale[:, c:c + 1],
                                                              ff_bank(u, ff_m, piece)[:, (2 + i) * P:(3 + i) * P], ALU.mult, ALU.mult)
                    last.then_inc(fuse_ready, 1)
                if is_tile(u, ff_m) and piece is None:
                    dve.wait_ge(down_made, tile(u, ff_m) + 1)
                    dve.wait_ge(fuse_lo_ready, tile(u, ff_m) * 3 + 3)
                    nc.vector.tensor_tensor(down_y, ff_bank(u, ff_m, piece)[:, 0:HID], down_rows[:, :], ALU.mult)\
                        .then_inc(down_scaled, 1)

                if at_step(u, k) == -GROUPS:
                    tables()
                if at_step(u, k) == -1:
                    scales()
                for kind, i in SPLIT_AT.get(at_step(u, k), ()):
                    if kind != "o":
                        weight_lo(kind, i)

                if is_tile(u, m + 1):
                    t1 = tile(u, m + 1)
                    if j == 0:
                        dve.wait_ge(kc_squared, t1 + 1)
                        if is_tile(u, m):
                            dve.wait_ge(ks_inv_ready, t1)
                        nc.vector.tensor_scalar(k_var[:, :], k_ssq[:, :], 1.0 / DIM, RMS_EPS, ALU.mult, ALU.add)\
                            .then_inc(kc_var_ready, 1)
                    if j == 1:
                        dve.wait_ge(ks_squared, t1 + 1)
                        nc.vector.tensor_scalar(k_var[:, :], k_ssq[:, :], 1.0 / DIM, RMS_EPS, ALU.mult, ALU.add)\
                            .then_inc(ks_var_ready, 1)
                        dve.wait_ge(kc_turned, t1 + 1)
                        nc.vector.tensor_tensor(k_cos[:, :, :], four(kv_bank(u, m + 1, j)), over_heads(rope[:, 2, :]), ALU.mult)
                        nc.vector.tensor_tensor(halves(k_sin[:, :, :]), rotated(four(kv_bank(u, m + 1, j))),
                                                halves(over_heads(rope[:, 3, :])), ALU.mult).then_inc(ks_roped, 1)
                    if j == 2:
                        dve.wait_ge(vc_hi_ready, t1 + 1)
                        for c in range(2):
                            rows = slice(c * LEN, (c + 1) * LEN)
                            last = nc.vector.tensor_tensor(v_lo[rows, nxt, 1 - c, :], kv_bank(u, m + 1, j)[rows, :],
                                                           as_f32(v_hi[rows, nxt, 1 - c, :]), ALU.subtract)
                        last.then_inc(vc_lo_ready, 1)
                    if j == 3:
                        dve.wait_ge(vs_hi_ready, t1 + 1)
                        for r in range(2):
                            rows = slice(r * LEN, (r + 1) * LEN)
                            last = nc.vector.tensor_tensor(v_lo[rows, nxt, r, :], kv_bank(u, m + 1, j)[rows, :],
                                                           as_f32(v_hi[rows, nxt, r, :]), ALU.subtract)
                        last.then_inc(vs_lo_ready, 1)

                if j == 0 and is_tile(u, m - 1):
                    count = tile(u, m - 1) + 1
                    dve.wait_ge(y_made, step(u, k - 1) + 1)
                    if is_tile(u, m - 3):
                        dve.wait_ge(out_stored[nxt], (u + (m - 3) // 2 + 1) * 32)
                    nc.vector.scalar_tensor_tensor(x1[:, nxt, :], ps_y[:, 0:HID], tanh_gates[:, 0:1], x_tile(u, m - 1),
                                                   ALU.mult, ALU.add).then_inc(x1_ready, 1)
                    dve.wait_ge(x1_ready, count)
                    nc.vector.bn_stats(x2_stats[:, :], x1[:, nxt, :]).then_inc(x2_counted, 1)
                    dve.wait_ge(x2_counted, count)
                if j == 1 and is_tile(u, m - 1):
                    dve.wait_ge(x2_inv_ready, tile(u, m - 1) + 1)
                    if is_tile(u, m + 1):
                        dve.wait_ge(xc_turned, tile(u, m + 1) + 1)
                    nc.vector.tensor_scalar(x2n[:, :], x1[:, nxt, :], x2_mean[:, 0:1], x2_inv[:, 0:1],
                                            ALU.subtract, ALU.mult).then_inc(x2_ready, 1)

                if isinstance(u, int) and step(u, k) == 0:
                    down_row_scale()
                if at_step(u, k) in ROUND_AT:
                    round_weights(ROUND_AT[step(u, k)])

                if is_step(u, k):
                    dve.wait_ge(pt_hi_ready, step(u, k) + 1)
                    nc.vector.tensor_tensor(pt_lo[:, :], ps_p[:, :], as_f32(pt_hi[:, :]), ALU.subtract)\
                        .then_inc(pt_lo_ready, 1)

                if j == 0 and is_tile(u, m - 1):
                    count = tile(u, m - 1) + 1
                    nc.vector.bn_aggr(x2_mean[:, :], x2_stats[:, :]).then_inc(x2_averaged, 1)
                    dve.wait_ge(x2_averaged, count)
                    if is_tile(u, m - 2):
                        dve.wait_ge(x2_inv_ready, count - 1)
                    nc.vector.tensor_scalar(x2_var[:, :], x2_mean[:, 1:2], LN_EPS, FF_IN_SCALE ** -2, ALU.add, ALU.mult)\
                        .then_inc(x2_var_ready, 1)

                if at_step(u, k) in ROUND_AT:
                    out_of_range(ROUND_AT[step(u, k)])

            run_steps(dve, one_step)

        @block.gpsimd
        def _(pool):
            def inverse_root(dst, src):
                return nc.gpsimd.tensor_tensor(dst, src, minus_half[:, 0:src.shape[1]], ALU.pow)

            def wo_lo(g):
                n = CHUNKS.index(("o", g))
                pool.wait_ge(wo_hi_ready, g + 1)
                nc.gpsimd.tensor_tensor(w_o[1][:, g].rearrange("p h n -> p (h n)"), staged(n, CHUNK_COLS),
                                        w_o[0][:, g].rearrange("p h n -> p (h n)").bitcast(f32), ALU.subtract)\
                    .then_inc(wo_lo_ready, 1)

            def quantize_store(i):
                kind, c = FF_CHUNKS[i]
                pool.wait_ge(quant_nan, i + 1)
                if kind == "down":
                    dst = w_down[:, c * (FC // 2):(c + 1) * (FC // 2), :].rearrange("p c n -> p (c n)")
                else:
                    dst = w_ff[:, ("gate", "up").index(kind), c, :]
                nc.gpsimd.tensor_tensor(dst, staged(CHUNKS.index(FF_CHUNKS[i]), FF), quant_m[:, :], ALU.add)\
                    .then_inc(quant_done, 1)

            def one_step(u, k):
                m, j = divmod(k, GROUPS)

                if is_step(u, k + 1):
                    pool.wait_ge(q_sin_ready, step(u, k + 1) + 1)
                    nc.gpsimd.tensor_tensor(q_rot[:, :, :], q_rot[:, :, :], q_sin[:, :, :], ALU.add)\
                        .then_inc(q_rot_ready, 1)
                    pool.wait_ge(ssq_moved, step(u, k + 1) + 1)
                    if is_step(u, k - 1):
                        pool.wait_ge(exp_ready, step(u, k - 1) + 1)
                    inverse_root(q_scale[:, (k + 1) % 2, :], ssq_rows[:, :]).then_inc(q_scale_ready, 1)

                if is_step(u, k):
                    pool.wait_ge(inv_ready, step(u, k) + 1)
                    nc.gpsimd.tensor_tensor(probs[:, :, :], probs[:, :, :], row_inv[:, :].unsqueeze(2).broadcast_to([P, 4, P]),
                                            ALU.mult).then_inc(probs_ready, 1)

                piece, ff_m = {2: (0, m - 1), 3: (1, m - 1), 0: (2, m - 2), 1: (None, m - 2)}[j]
                if is_tile(u, ff_m) and piece is not None:
                    count = tile(u, ff_m) * 3 + piece + 1
                    hi = fuse_hi[:, 2 * piece:2 * piece + 2, :]
                    pool.wait_ge(fuse_hi_ready, count)
                    nc.gpsimd.tensor_tensor(fuse_lo[:, 2 * piece:2 * piece + 2, :], fuse[:, :, :], hi.bitcast(f32),
                                            ALU.subtract).then_inc(fuse_lo_ready, 1)
                if is_tile(u, ff_m) and piece is None:
                    pool.wait_ge(down_scaled, tile(u, ff_m) + 1)
                    nc.gpsimd.tensor_tensor(x1[:, m % 2, :], down_y, x1[:, m % 2, :], ALU.add)\
                        .then_inc(result_ready, 1)

                if is_tile(u, m + 1):
                    t1 = tile(u, m + 1)
                    if j == 0:
                        pool.wait_ge(kc_var_ready, t1 + 1)
                        if is_tile(u, m):
                            pool.wait_ge(ks_ready, t1)
                        inverse_root(k_inv[:, :], k_var[:, :]).then_inc(kc_inv_ready, 1)
                    if j == 1:
                        pool.wait_ge(ks_var_ready, t1 + 1)
                        pool.wait_ge(kc_ready, t1 + 1)
                        inverse_root(k_inv[:, :], k_var[:, :]).then_inc(ks_inv_ready, 1)
                        pool.wait_ge(ks_roped, t1 + 1)
                        nc.gpsimd.tensor_tensor(k_cos[:, :, :], k_cos[:, :, :], k_sin[:, :, :], ALU.add)\
                            .then_inc(ks_added, 1)
                        pool.wait_ge(ks_added, t1 + 1)
                        pool.wait_ge(ks_inv_ready, t1 + 1)
                        nc.gpsimd.tensor_tensor(kn[:, :, :], k_cos[:, :, :],
                                                k_inv[:, :].unsqueeze(2).broadcast_to([P, HPG, DIM]), ALU.mult)\
                            .then_inc(ks_ready, 1)

                if j == 2 and is_tile(u, m + 2):
                    pool.wait_ge(ln_var_ready, tile(u, m + 2) + 1)
                    if is_tile(u, m + 1):
                        pool.wait_ge(xn_ready, tile(u, m + 1) + 1)
                    inverse_root(ln_inv[:, :], ln_var[:, :]).then_inc(ln_inv_ready, 1)
                if j == 0 and is_tile(u, m - 1):
                    pool.wait_ge(x2_var_ready, tile(u, m - 1) + 1)
                    if is_tile(u, m - 2):
                        pool.wait_ge(x2_ready, tile(u, m - 2) + 1)
                    inverse_root(x2_inv[:, :], x2_var[:, :]).then_inc(x2_inv_ready, 1)

                for kind, i in SPLIT_AT.get(at_step(u, k), ()):
                    if kind == "o":
                        wo_lo(i)
                if at_step(u, k) in ROUND_AT:
                    quantize_store(ROUND_AT[step(u, k)])

            nc.gpsimd.memset(minus_half[:, :], -0.5).then_inc(half_set, 1)
            pool.wait_ge(half_set, 1)
            run_steps(pool, one_step)


_INS = ["x", "ctx_2048", "g_xattn", "g_ffn", "L0_xattn_wq", "L0_xattn_wk", "L0_xattn_wv", "L0_xattn_wo",
        "L0_xattn_wk_ctx", "L0_xattn_wv_ctx", "L0_xattn_q_norm_w", "L0_xattn_k_norm_w", "L0_ffn_gate_w",
        "L0_ffn_up_w", "L0_ffn_down_w", "L0_ffn_gate_scale", "L0_ffn_up_scale", "L0_ffn_down_scale"]


def shape_constants():
    inv_freq = (1.0 / 10000.0 ** (np.arange(0, DIM, 2, dtype=np.float32) / DIM)).astype(np.float32)
    angles = np.outer(np.arange(LEN, dtype=np.float32), inv_freq)
    angles = np.concatenate([angles, angles], -1)
    sign = np.where(np.arange(DIM) < HALF, -1.0, 1.0).astype(np.float32)
    table = np.zeros((P, C_ALL), np.float32)
    table[:, C_COS:C_COS + DIM] = np.tile(np.cos(angles), (2, 1))
    table[:, C_SIN:C_SIN + DIM] = np.tile(np.sin(angles) * sign, (2, 1))
    late = np.arange(LEN)[None, :] > np.arange(LEN)[:, None]
    table[:, C_MASK:C_MASK + LEN] = np.tile(np.where(late, MASKED, 0.0), (2, 1))
    table[:, C_ID:C_ID + P] = np.eye(P)
    return table


def kernel(**inputs):
    import concourse.bacc as bacc
    from concourse.bass_utils import run_bass_kernel_spmd

    nc = bacc.Bacc("TRN2", target_bir_lowering=False, num_devices=1)
    arrays, args = {}, []
    given = [(name, np.ascontiguousarray(inputs[name])) for name in _INS] + [("constants", shape_constants())]
    for name, a in given:
        arrays[f"in_{name}_dram"] = a
        args.append(nc.dram_tensor(f"in_{name}_dram", a.shape, mybir.dt.from_np(a.dtype), kind="ExternalInput").ap())
    args.append(nc.dram_tensor("out_0_dram", (BATCHES, LEN, HID), mybir.dt.float32, kind="ExternalOutput").ap())
    build(nc, *args)
    r = run_bass_kernel_spmd(nc, [arrays], core_ids=[0])
    return r.results[0]["out_0_dram"]
```

```python
import math
from contextlib import ExitStack

import numpy as np

import concourse.bass as bass
from concourse import mybir

BATCHES, LEN, HID = 16, 64, 256
HEADS, GROUPS, DIM = 16, 4, 128
FF = 768
P = 128
TILES = BATCHES // 2
STEPS = TILES * GROUPS
HPG = HEADS // GROUPS
GW = HPG * DIM
KC = HID // P
FC = FF // P
HALF = DIM // 2

LN_EPS = 1e-5
RMS_EPS = 1e-6
MASKED = -1e30
FF_IN_SCALE = 64.0

E4M3_MIN_NORMAL = 2.0 ** -6
E4M3_ROUNDER = 1.5 * 2.0 ** 20
E4M3_OVERFLOW = 2.0 ** 120 / 460.0 * 256.0
EXPONENT_BITS = 0x7F800000

C_COS, C_SIN, C_MASK, C_ID, C_ALL = 0, DIM, 2 * DIM, 2 * DIM + LEN, 2 * DIM + LEN + P

KV_KINDS = ("k_ctx", "k_self", "v_ctx", "v_self")
CHUNKS = [("kv", 0), ("kv", 1), ("kv", 2), ("q", 0), ("kv", 3), ("q", 1), ("q", 2), ("o", 0), ("q", 3),
          ("gate", 0), ("o", 1), ("gate", 1), ("o", 2), ("o", 3), ("up", 0), ("up", 1), ("down", 0), ("down", 1)]
FF_CHUNKS = [c for c in CHUNKS if c[0] in ("gate", "up", "down")]
SPLIT_AT = {-4: [("kv", 0), ("kv", 1), ("kv", 2)], -3: [("q", 0)], -2: [("kv", 3)], -1: [("q", 1)],
            0: [("q", 2), ("o", 0)], 1: [("q", 3), ("o", 1)], 2: [("o", 2)], 3: [("o", 3)]}
SPLIT_ORDER = [c for at in sorted(SPLIT_AT) for c in SPLIT_AT[at] if c[0] != "o"]
ROUND_AT = {0: 0, 2: 1, 3: 2, 4: 3, 5: 4, 6: 5}
SHORT_OF_VECTOR = (3,)
TABLES_AHEAD_OF = ("kv", 2)
RING = 4
CHUNK_COLS = 1024

FIRST_STEP, LAST_STEP = -6, STEPS + 7


def build(nc, x, ctx_in, g_xattn, g_ffn, wq, wk, wv, wo, wk_ctx, wv_ctx, q_norm_w, k_norm_w,
          gate_w, up_w, down_w, gate_scale, up_scale, down_scale, constants, out):
    f32, f32r, f16, bf16, u32 = (mybir.dt.float32, mybir.dt.float32r, mybir.dt.float16, mybir.dt.bfloat16,
                                 mybir.dt.uint32)
    ALU, ACT, AX = mybir.AluOpType, mybir.ActivationFunctionType, mybir.AxisListType

    with ExitStack() as stack:
        def sb(name, shape, dt=f32):
            return stack.enter_context(nc.sbuf_tensor(name, shape, dt))

        def bank(name):
            return stack.enter_context(nc.psum_tensor(name, [P, 512], f32))

        def sem(name):
            return stack.enter_context(nc.semaphore(name))

        const = sb("const", [P, C_ALL])
        mask = sb("mask", [P, LEN], bf16)
        ident_bf = sb("ident_bf", [P, P], bf16)
        ident = const[:, C_ID:C_ID + P]
        minus_half = sb("minus_half", [P, HPG])
        rope = sb("rope", [P, 4, DIM])
        k_w_col = sb("k_w_col", [P, 1])
        gates = sb("gates", [P, 2])
        tanh_gates = sb("tanh_gates", [P, 2])
        ff_rows = sb("ff_rows", [2 * FC, P])
        ff_scales = sb("ff_scales", [P, 2, FC])
        tanh_scale = sb("tanh_scale", [P, FC])
        fuse_scale = sb("fuse_scale", [P, FC])
        down_rows = sb("down_rows", [P, HID])

        x_sb = sb("x_sb", [P, TILES, HID])
        ctx_sb = sb("ctx_sb", [P, 2, HID])
        xn = sb("xn", [P, HID])
        stage = sb("stage", [P, RING, CHUNK_COLS])
        w_kv = [sb(f"w_kv_{a}", [P, 4, KC, GW], f32r) for a in ("hi", "lo")]
        w_q = [sb(f"w_q_{a}", [P, GROUPS, KC, GW], f32r) for a in ("hi", "lo")]
        w_o = [sb(f"w_o_{a}", [P, GROUPS, HPG, HID], f32r) for a in ("hi", "lo")]
        w_ff = sb("w_ff", [P, 2, KC, FF], f16)
        w_down = sb("w_down", [P, FC, HID], f32r)
        quant_m = sb("quant_m", [P, FF])

        xt = [sb(f"xt_{a}", [P, 2, 2 * KC, P], f32r) for a in ("hi", "lo")]
        kt = sb("kt", [P, 2, GROUPS, 4, LEN])
        v_hi = sb("v_hi", [P, 2, 2, GW], f32r)
        v_lo = sb("v_lo", [P, 2, 2, GW], f32r)
        q_rot = sb("q_rot", [P, HPG, DIM])
        q_sin = sb("q_sin", [P, HPG, DIM])
        qt = sb("qt", [P, 2, HPG, LEN])
        k_cos = sb("k_cos", [P, HPG, DIM])
        k_sin = sb("k_sin", [P, HPG, DIM])
        kn = k_sin
        probs = sb("probs", [P, 4, P])
        pt_hi = sb("pt_hi", [P, 512], f32r)
        pt_lo = sb("pt_lo", [P, 512], f32r)
        ot_hi = sb("ot_hi", [P, HPG, P], f32r)
        ot_lo = sb("ot_lo", [P, HPG, P], f32r)
        squares = const[:, 0:2 * DIM].bitcast(bf16).rearrange("p (h d) -> p h d", h=HPG)

        ssq = sb("ssq", [P, HPG])
        ssq_rows = sb("ssq_rows", [P, 4])
        q_scale = sb("q_scale", [P, 2, 4])
        row_max = sb("row_max", [P, 4])
        exp_bias = sb("exp_bias", [P, 4])
        row_sum = sb("row_sum", [P, 4])
        row_inv = sb("row_inv", [P, 4])
        k_ssq = sb("k_ssq", [P, HPG])
        k_var = sb("k_var", [P, HPG])
        k_inv = sb("k_inv", [P, HPG])
        ln_stats = sb("ln_stats", [P, 6])
        ln_mean = sb("ln_mean", [P, 2])
        ln_var = sb("ln_var", [P, 1])
        ln_inv = sb("ln_inv", [P, 1])
        x2_stats = sb("x2_stats", [P, 6])
        x2_mean = sb("x2_mean", [P, 2])
        x2_var = sb("x2_var", [P, 1])
        x2_inv = sb("x2_inv", [P, 1])

        x1 = sb("x1", [P, 2, HID])
        x2n = xn
        x2t = [sb(f"x2t_{a}", [P, KC, P], f16) for a in ("hi", "lo")]
        tanh_g = sb("tanh_g", [P, 2, P])
        fuse = sb("fuse", [P, 2, P])
        fuse_hi = sb("fuse_hi", [P, FC, P], f32r)
        fuse_lo = sb("fuse_lo", [P, FC, P], f32r)
        down_y = fuse[:, :, :].rearrange("p a n -> p (a n)")

        ps_t, ps_q, ps_s, ps_o, ps_f, ps_k, ps_y, ps_p = (
            bank(n) for n in ("ps_transposed", "ps_q", "ps_scores", "ps_attn", "ps_ff", "ps_kv", "ps_y", "ps_probs"))

        const_in, small_in, late_in, x0_in, x_in = (
            sem(n) for n in ("const_in", "small_in", "late_in", "x0_in", "x_in"))
        ctx_in_sem = [sem(f"ctx_in_{i}") for i in range(2)]
        chunk_in = [sem(f"chunk_in_{i}") for i in range(len(CHUNKS))]
        x1_free = [sem(f"x1_free_{i}") for i in range(2)]
        half_set = sem("half_set")
        tables_ready = sem("tables_ready")
        gates_ready = sem("gates_ready")
        scales_turned, scales_copied, scales_ready = sem("scales_turned"), sem("scales_copied"), sem("scales_ready")
        w_hi_ready, w_lo_ready = sem("w_hi_ready"), sem("w_lo_ready")
        wo_hi_ready, wo_lo_ready = sem("wo_hi_ready"), sem("wo_lo_ready")
        quant_exp, quant_round, quant_sum, quant_diff, quant_nan, quant_done = (
            sem(n) for n in ("quant_exp", "quant_round", "quant_sum", "quant_diff", "quant_nan", "quant_done"))
        ln_counted, ln_averaged, ln_var_ready, ln_inv_ready, xn_ready = (
            sem(n) for n in ("ln_counted", "ln_averaged", "ln_var_ready", "ln_inv_ready", "xn_ready"))
        xc_turned, xt_hi_ready, xt_lo_ready = sem("xc_turned"), sem("xt_hi_ready"), sem("xt_lo_ready")
        kv_made = {kind: sem(f"{kind}_made") for kind in KV_KINDS}
        kc_squared, kc_var_ready, kc_inv_ready, kc_ready, kc_turned, kc_stored = (
            sem(n) for n in ("kc_squared", "kc_var_ready", "kc_inv_ready", "kc_ready", "kc_turned", "kc_stored"))
        ks_squared, ks_var_ready, ks_inv_ready, ks_roped, ks_added, ks_ready, ks_turned, ks_stored = (
            sem(n) for n in ("ks_squared", "ks_var_ready", "ks_inv_ready", "ks_roped", "ks_added", "ks_ready",
                             "ks_turned", "ks_stored"))
        vc_hi_ready, vc_lo_ready, vs_hi_ready, vs_lo_ready = (
            sem(n) for n in ("vc_hi_ready", "vc_lo_ready", "vs_hi_ready", "vs_lo_ready"))
        x1_ready, x2_counted, x2_averaged, x2_var_ready, x2_inv_ready, x2_ready, x2_turned, x2_hi_ready, x2_lo_ready = (
            sem(n) for n in ("x1_ready", "x2_counted", "x2_averaged", "x2_var_ready", "x2_inv_ready", "x2_ready",
                             "x2_turned", "x2_hi_ready", "x2_lo_ready"))
        ff_made, tanh_ready, gated_ready, fuse_ready, fuse_hi_ready, fuse_lo_ready = (
            sem(n) for n in ("ff_made", "tanh_ready", "gated_ready", "fuse_ready", "fuse_hi_ready", "fuse_lo_ready"))
        down_made, down_scaled, result_ready = sem("down_made"), sem("down_scaled"), sem("result_ready")
        q_made, q_squared, q_cos_ready, q_sin_ready, q_rot_ready, ssq_moved, q_scale_ready, q_turned, qt_ready = (
            sem(n) for n in ("q_made", "q_squared", "q_cos_ready", "q_sin_ready", "q_rot_ready", "ssq_moved",
                             "q_scale_ready", "q_turned", "qt_ready"))
        scores_made, max_ready, bias_ready, exp_ready, inv_ready, probs_ready, probs_turned, pt_hi_ready, pt_lo_ready = (
            sem(n) for n in ("scores_made", "max_ready", "bias_ready", "exp_ready", "inv_ready", "probs_ready",
                             "probs_turned", "pt_hi_ready", "pt_lo_ready"))
        attn_made, ot_hi_ready, ot_lo_ready, y_made = (
            sem(n) for n in ("attn_made", "ot_hi_ready", "ot_lo_ready", "y_made"))

        def step(u, k):
            return u * (2 * GROUPS) + k

        def tile(u, m):
            return u * 2 + m

        def is_step(u, k):
            return not isinstance(u, int) or 0 <= step(u, k) < STEPS

        def is_tile(u, m):
            return not isinstance(u, int) or 0 <= tile(u, m) < TILES

        def run_steps(eng, one_step):
            for k in range(FIRST_STEP, 2 * GROUPS):
                one_step(0, k)
            with eng.Fori(1, TILES // 2 - 1) as u:
                for k in range(2 * GROUPS):
                    one_step(u, k)
            last = TILES // 2 - 1
            for k in range(LAST_STEP - step(last, 0)):
                one_step(last, k)

        def at_step(u, k):
            return step(u, k) if isinstance(u, int) else None

        def kv_bank(u, m, j):
            return (ps_k, ps_f, ps_o, ps_p)[j] if first_tile(u, m) else ps_k

        def ff_bank(u, m, piece):
            return {0: ps_f, 1: ps_k, 2: ps_s, None: ps_q}[piece] if last_tile(u, m) else ps_f

        def piece_at(m, j):
            return {2: (0, m - 1), 3: (1, m - 1), 0: (2, m - 2), 1: (None, m - 2)}[j]

        def piece_before(m, j):
            return piece_at(m, j - 1) if j else piece_at(m - 1, GROUPS - 1)

        def projects_late(u, k):
            return isinstance(u, int) and (step(u, k) < 2 * GROUPS or step(u, k) >= STEPS - GROUPS)

        def tanh_part(u, m, piece):
            if last_tile(u, m) and piece:
                return probs[:, 2 * piece - 2:2 * piece, :]
            return tanh_g[:, :, :]

        def fuse_part(u, m, piece):
            if last_tile(u, m) and piece:
                return k_cos[:, 2 * piece - 2:2 * piece, :]
            return fuse[:, :, :]

        def first_tile(u, m):
            return isinstance(u, int) and tile(u, m) == 0

        def last_tile(u, m):
            return isinstance(u, int) and tile(u, m) == TILES - 1

        def four(ap):
            return ap[:, :].rearrange("p (h d) -> p h d", h=4)

        def rotated(ap):
            return ap.rearrange("p h (f j) -> p h f j", f=2)[:, :, ::-1, :]

        def halves(ap):
            return ap.rearrange("p h (f j) -> p h f j", f=2)

        def over_heads(row):
            return row.unsqueeze(1).broadcast_to([P, HPG, DIM])

        def staged(n, cols):
            return stage[:, n % RING, 0:cols]

        block = stack.enter_context(nc.Block())

        @block.sync
        def _(sp):
            x_by_half = x.rearrange("(t c) l n -> c l t n", c=2)
            out_by_half = out.rearrange("(t c) l n -> c l t n", c=2)
            ctx_rows = ctx_in.rearrange("(t c) l n -> (c l) t n", c=2)
            kv_views = [w.rearrange("(c p) n -> p c n", p=P) for w in (wk_ctx, wk, wv_ctx, wv)]
            wq_view = wq.rearrange("(c p) (g n) -> p g c n", p=P, g=GROUPS)
            wo_view = wo.rearrange("(g h p) n -> p g h n", p=P, g=GROUPS)
            ff_views = {"gate": gate_w, "up": up_w}
            down_view = down_w.rearrange("(c p) n -> p c n", p=P)

            def load_chunk(n):
                kind, i = CHUNKS[n]
                if n >= RING:
                    before = n - RING
                    kind_before, i_before = CHUNKS[before]
                    if kind_before == "o":
                        sp.wait_ge(wo_lo_ready, i_before + 1)
                    elif kind_before in ("kv", "q"):
                        sp.wait_ge(w_lo_ready, SPLIT_ORDER.index(CHUNKS[before]) + 1)
                    else:
                        sp.wait_ge(quant_done, FF_CHUNKS.index(CHUNKS[before]) + 1)
                if kind == "kv":
                    sp.dma_start(staged(n, CHUNK_COLS).rearrange("p (c n) -> p c n", c=KC), kv_views[i])\
                      .then_inc(chunk_in[n], 16)
                elif kind == "q":
                    sp.dma_start(staged(n, CHUNK_COLS).rearrange("p (c n) -> p c n", c=KC), wq_view[:, i])\
                      .then_inc(chunk_in[n], 16)
                elif kind == "o":
                    sp.dma_start(staged(n, CHUNK_COLS).rearrange("p (h n) -> p h n", h=HPG), wo_view[:, i])\
                      .then_inc(chunk_in[n], 16)
                elif kind == "down":
                    sp.dma_start(staged(n, FF).rearrange("p (c n) -> p c n", c=FC // 2),
                                 down_view[:, i * (FC // 2):(i + 1) * (FC // 2), :]).then_inc(chunk_in[n], 16)
                else:
                    sp.dma_start(staged(n, FF), ff_views[kind][i * P:(i + 1) * P, :]).then_inc(chunk_in[n], 16)

            for r in range(2):
                sp.dma_start(x_sb[r * LEN:(r + 1) * LEN, 0, :], x_by_half[1 - r][:, 0, :]).then_inc(x0_in, 16)
            sp.dma_start(ctx_sb[:, 0, :], ctx_rows[:, 0, :]).then_inc(ctx_in_sem[0], 16)
            sp.dma_start(const[:, :], constants).then_inc(const_in, 16)
            load_chunk(0)
            load_chunk(1)
            for n, w in enumerate((q_norm_w, k_norm_w)):
                row = w.rearrange("(a d) -> a d", a=1)
                sp.dma_start(rope[:, 2 * n, :], row.broadcast_to([P, DIM])).then_inc(small_in, 16)
                for f in range(2):
                    sp.dma_start(rope[:, 2 * n + 1, f * HALF:(f + 1) * HALF],
                                 row[:, (1 - f) * HALF:(2 - f) * HALF].broadcast_to([P, HALF])).then_inc(small_in, 16)
            sp.dma_start(k_w_col[:, :], k_norm_w.rearrange("(d a) -> d a", a=1)).then_inc(small_in, 16)
            for n in range(2, RING):
                load_chunk(n)
            for n, w in enumerate((g_xattn, g_ffn)):
                sp.dma_start(gates[:, n:n + 1], w.rearrange("(a n) -> a n", a=1).broadcast_to([P, 1]))\
                  .then_inc(late_in, 16)
            for n, w in enumerate((gate_scale, up_scale)):
                sp.dma_start(ff_rows[n * FC:(n + 1) * FC, :], w.rearrange("(c p) -> c p", p=P)).then_inc(late_in, 16)
            sp.dma_start(down_rows[:, :], down_scale.rearrange("(a n) -> a n", a=1).broadcast_to([P, HID]))\
              .then_inc(late_in, 16)
            sp.dma_start(ctx_sb[:, 1, :], ctx_rows[:, 1, :]).then_inc(ctx_in_sem[1], 16)
            for n in range(RING, RING + 2):
                load_chunk(n)
            def load_context(u, m):
                sp.wait_ge(xc_turned, tile(u, m) + 1)
                sp.dma_start(ctx_sb[:, m, :].unsqueeze(1), ctx_rows[:, bass.ds(tile(u, m + 2), 1), :])\
                  .then_inc(ctx_in_sem[m], 16)

            def store_tile(u, m):
                sp.wait_ge(result_ready, tile(u, m) + 1)
                for r in range(2):
                    sp.dma_start(out_by_half[1 - r][:, bass.ds(tile(u, m), 1), :],
                                 x1[r * LEN:(r + 1) * LEN, m % 2, :].unsqueeze(1)).then_inc(x1_free[m % 2], 16)

            load_context(0, 0)
            for r in range(2):
                sp.dma_start(x_sb[r * LEN:(r + 1) * LEN, 1:TILES, :], x_by_half[1 - r][:, 1:TILES, :])\
                  .then_inc(x_in, 16)
            for n in range(RING + 2, len(CHUNKS)):
                if n == CHUNKS.index(("o", 1)):
                    load_context(0, 1)
                load_chunk(n)
            with sp.Fori(1, TILES // 2 - 1) as u:
                for m in range(2):
                    load_context(u, m)
                for m in range(2):
                    store_tile(u, m - 2)
            for m in range(2 * 2):
                store_tile(TILES // 2, m - 2 * 2)
            for m in range(2):
                sp.wait_ge(x1_free[m], 32 * (TILES // 2 + 1))

        @block.tensor
        def _(pe):
            def three_passes(dst, lhs, rhs, terms):
                n, passes = 0, [(0, 0), (0, 1), (1, 0)]
                for i in range(terms):
                    for a, b in passes:
                        last = nc.tensor.matmul(dst, lhs(a, i), rhs(b, i), start=(n == 0),
                                                stop=(n == 3 * terms - 1))
                        n += 1
                return last

            def turn(dst, srcs):
                for i, src in enumerate(srcs):
                    last = nc.tensor.matmul(dst[:, i * P:(i + 1) * P], src, ident, start=True, stop=True,
                                            is_transpose=True)
                return last

            def output_projection(u, k):
                m, j = divmod(k, GROUPS)
                if is_step(u, k - 2):
                    g0 = (k - 2) % GROUPS
                    m0 = (k - 2) // GROUPS
                    pe.wait_ge(ot_lo_ready, step(u, k - 2) + 1)
                    if isinstance(u, int) and 0 <= step(u, k - 2) < GROUPS:
                        pe.wait_ge(wo_lo_ready, g0 + 1)
                    if g0 == 0 and is_tile(u, m0 - 1):
                        pe.wait_ge(x1_ready, tile(u, m0))
                    ot = (ot_hi, ot_lo)
                    n = 0
                    for h in range(HPG):
                        for a, b in ((0, 0), (0, 1), (1, 0)):
                            last = nc.tensor.matmul(ps_y[:, 0:HID], ot[a][:, h, :], w_o[b][:, g0, h, :],
                                                    start=(g0 == 0 and n == 0),
                                                    stop=(g0 == GROUPS - 1 and n == 3 * HPG - 1))
                            n += 1
                    last.then_inc(y_made, 1)

            def turn_context_keys(u, k):
                m, j = divmod(k, GROUPS)
                if j == 1 and is_tile(u, m + 1):
                    pe.wait_ge(kc_ready, tile(u, m + 1) + 1)
                    turn(ps_t, [kn[:, h, :] for h in range(GROUPS)]).then_inc(kc_turned, 1)

            def feed_forward(u, m, j):
                piece, ff_m = piece_at(m, j)
                if is_tile(u, ff_m) and piece is not None:
                    pe.wait_ge(x2_lo_ready, tile(u, ff_m) + 1)
                    if isinstance(u, int) and tile(u, ff_m) == 0:
                        pe.wait_ge(quant_done, 4)
                    if piece == 0 and is_tile(u, ff_m - 1):
                        pe.wait_ge(down_scaled, tile(u, ff_m))
                    elif piece > 0 and not last_tile(u, ff_m):
                        pe.wait_ge(fuse_ready, tile(u, ff_m) * 3 + piece)
                    bank_f = ff_bank(u, ff_m, piece)
                    for i, (w, c) in enumerate(((0, 2 * piece), (0, 2 * piece + 1), (1, 2 * piece), (1, 2 * piece + 1))):
                        n = 0
                        for kc in range(KC):
                            for a in range(2):
                                last = nc.tensor.matmul(bank_f[:, i * P:(i + 1) * P],
                                                        w_ff[:, w, kc, c * P:(c + 1) * P], x2t[a][:, kc, :],
                                                        start=(n == 0), stop=(n == 2 * KC - 1))
                                n += 1
                    last.then_inc(ff_made, 1)
                if is_tile(u, ff_m) and piece is None:
                    if isinstance(u, int) and tile(u, ff_m) == 0:
                        pe.wait_ge(quant_done, 6)
                    if not last_tile(u, ff_m):
                        pe.wait_ge(fuse_ready, tile(u, ff_m) * 3 + 3)
                        pe.wait_ge(fuse_lo_ready, tile(u, ff_m) * 3 + 3)
                    for c in range(FC):
                        if last_tile(u, ff_m) and c % 2 == 0:
                            pe.wait_ge(fuse_hi_ready, tile(u, ff_m) * 3 + c // 2 + 1)
                            pe.wait_ge(fuse_lo_ready, tile(u, ff_m) * 3 + c // 2 + 1)
                        for a, part in enumerate((fuse_hi, fuse_lo)):
                            last = nc.tensor.matmul(ff_bank(u, ff_m, piece)[:, 0:HID], part[:, c, :], w_down[:, c, :],
                                                    start=(c == 0 and a == 0), stop=(c == FC - 1 and a == 1))
                    last.then_inc(down_made, 1)

            def keys_values(u, k):
                m, j = divmod(k, GROUPS)
                par, nxt = m % 2, (m + 1) % 2
                if is_tile(u, m + 1):
                    kind = KV_KINDS[j]
                    t1 = tile(u, m + 1)
                    pe.wait_ge(xt_lo_ready, t1 + 1)
                    if isinstance(u, int) and t1 == 0:
                        split = SPLIT_ORDER.index(("kv", j)) + 1
                        pe.wait_ge(w_hi_ready, split)
                        pe.wait_ge(w_lo_ready, split)
                    if j == 0 and is_tile(u, m):
                        pe.wait_ge(vs_lo_ready, t1)
                    if j == 1 and not first_tile(u, m + 1):
                        pe.wait_ge(kc_ready, t1 + 1)
                    if j == 2 and not first_tile(u, m + 1):
                        pe.wait_ge(ks_squared, t1 + 1)
                    if j == 3 and not first_tile(u, m + 1):
                        pe.wait_ge(vc_lo_ready, t1 + 1)
                    base = KC if kind.endswith("ctx") else 0
                    three_passes(kv_bank(u, m + 1, j)[:, :], lambda a, i: xt[a][:, nxt, base + i, :],
                                 lambda b, i: w_kv[b][:, j, i, :], KC).then_inc(kv_made[kind], 1)

            def one_step(u, k):
                m, j = divmod(k, GROUPS)
                par, nxt = m % 2, (m + 1) % 2

                if is_step(u, k):
                    pe.wait_ge(q_rot_ready, step(u, k) + 1)
                    if j == 1 and is_tile(u, m + 1):
                        pe.wait_ge(xt_lo_ready, tile(u, m + 1) + 1)
                    if j == 2 and is_tile(u, m + 1):
                        pe.wait_ge(kc_stored, tile(u, m + 1) + 1)
                    if j == 3 and is_tile(u, m - 1):
                        pe.wait_ge(x2_lo_ready, tile(u, m - 1) + 1)
                    if j == 0:
                        pe.wait_ge(ks_stored, tile(u, m) + 1)
                    turn(ps_t, [q_rot[:, h, :] for h in range(HPG)]).then_inc(q_turned, 1)

                if is_step(u, k + 1):
                    g1 = (k + 1) % GROUPS
                    p1 = ((k + 1) // GROUPS) % 2
                    if isinstance(u, int) and 0 <= step(u, k + 1) < GROUPS:
                        split = SPLIT_ORDER.index(("q", step(u, k + 1))) + 1
                        pe.wait_ge(w_lo_ready, split)
                        pe.wait_ge(w_hi_ready, split)
                    pe.wait_ge(xt_lo_ready, tile(u, (k + 1) // GROUPS) + 1)
                    if is_step(u, k):
                        pe.wait_ge(q_sin_ready, step(u, k) + 1)
                    three_passes(ps_q[:, :], lambda a, i: xt[a][:, p1, i, :], lambda b, i: w_q[b][:, g1, i, :], KC)\
                        .then_inc(q_made, 1)

                if at_step(u, k) == -1:
                    keys_values(u, k - 1)

                if not projects_late(u, k):
                    output_projection(u, k)

                if is_step(u, k):
                    pe.wait_ge(qt_ready, step(u, k) + 1)
                if j == 0 and is_tile(u, m + 1):
                    pe.wait_ge(xn_ready, tile(u, m + 1) + 1)
                    if isinstance(u, int) and tile(u, m + 1) == 0:
                        pe.wait_ge(const_in, 16)
                    pe.wait_ge(ctx_in_sem[nxt], 16 * (u + (m + 1) // 2 + 1))
                    turn(ps_t, [xn[:, i * P:(i + 1) * P] for i in range(KC)]
                         + [ctx_sb[:, nxt, i * P:(i + 1) * P] for i in range(KC)]).then_inc(xc_turned, 1)
                if j == 2 and is_tile(u, m - 1):
                    pe.wait_ge(x2_ready, tile(u, m - 1) + 1)
                    turn(ps_t, [x2n[:, i * P:(i + 1) * P] for i in range(KC)]).then_inc(x2_turned, 1)
                if j == 3 and is_tile(u, m + 1):
                    pe.wait_ge(ks_ready, tile(u, m + 1) + 1)
                    turn(ps_t, [kn[:, h, :] for h in range(GROUPS)]).then_inc(ks_turned, 1)

                if is_step(u, k):
                    if j == 0:
                        pe.wait_ge(ks_stored, tile(u, m) + 1)
                    if isinstance(u, int) and step(u, k) == 0:
                        pe.wait_ge(tables_ready, 6)
                    scores = four(ps_s)
                    for r in range(2):
                        nc.tensor.matmul(scores[:, 2 * r:2 * r + 2, r * LEN:(r + 1) * LEN], ident_bf[:, :],
                                         mask[:, :].unsqueeze(1).broadcast_to([P, 2, LEN]),
                                         start=(r == 0), stop=False, skip_group_check=True)
                    for r in range(2):
                        for pp in range(2):
                            last = nc.tensor.matmul(scores[:, 2 * r + pp, :],
                                                    qt[:, r, 2 * pp:2 * pp + 2, :],
                                                    kt[:, par, j, 2 * r:2 * r + 2, :],
                                                    start=False, stop=(r == 1 and pp == 1), skip_group_check=True)
                    last.then_inc(scores_made, 1)

                if is_step(u, k - 1):
                    pe.wait_ge(probs_ready, step(u, k - 1) + 1)
                    turn(ps_p, [probs[:, i, :] for i in range(4)]).then_inc(probs_turned, 1)

                if at_step(u, k) == -2:
                    pe.wait_ge(late_in, 16 * 5)
                    nc.tensor.matmul(ps_y[:, 0:2 * FC], ff_rows[:, :], ident[0:2 * FC, 0:2 * FC], start=True, stop=True,
                                     is_transpose=True).then_inc(scales_turned, 1)

                if projects_late(u, k):
                    output_projection(u, k)

                if j in (0, 3) and at_step(u, k) != STEPS:
                    feed_forward(u, m, j)

                if not first_tile(u, m + 1):
                    turn_context_keys(u, k)

                if at_step(u, k) != -2:
                    keys_values(u, k)
                if first_tile(u, m + 1):
                    turn_context_keys(u, k)

                if j in (1, 2):
                    feed_forward(u, m, j)

                if is_step(u, k - 1):
                    g0, p0 = (k - 1) % GROUPS, ((k - 1) // GROUPS) % 2
                    pe.wait_ge(pt_lo_ready, step(u, k - 1) + 1)
                    if g0 == 0:
                        pe.wait_ge(vs_lo_ready, tile(u, (k - 1) // GROUPS) + 1)
                    for r in range(2):
                        v = (v_hi, v_lo)
                        pt = (pt_hi, pt_lo)
                        last = three_passes(ps_o[:, r * 256:(r + 1) * 256],
                                            lambda a, i: v[a][:, p0, r, g0 * DIM:(g0 + 1) * DIM],
                                            lambda b, i: pt[b][:, r * 256:(r + 1) * 256], 1)
                    last.then_inc(attn_made, 1)

                if at_step(u, k) == STEPS:
                    feed_forward(u, m, j)

            run_steps(pe, one_step)

        @block.scalar
        def _(act):
            def weight_hi(kind, i):
                n = CHUNKS.index((kind, i))
                act.wait_ge(chunk_in[n], 16)
                dst = {"kv": w_kv, "q": w_q, "o": w_o}[kind][0]
                nc.scalar.activation(dst[:, i].rearrange("p c n -> p (c n)"), staged(n, CHUNK_COLS), ACT.Copy)\
                    .then_inc(wo_hi_ready if kind == "o" else w_hi_ready, 1)

            def split_weights(u, k):
                for kind, i in SPLIT_AT.get(at_step(u, k), ()):
                    weight_hi(kind, i)

            def square_heads(src, dst):
                for h in range(HPG):
                    last = nc.scalar.activation(squares[:, h, :], src[:, h * DIM:(h + 1) * DIM], ACT.Square,
                                                accum_out=dst[:, h:h + 1])
                return last

            def fuse_high(u, k):
                m, j = divmod(k, GROUPS)
                piece, ff_m = piece_before(m, j)
                if is_tile(u, ff_m) and piece is not None:
                    act.wait_ge(fuse_ready, tile(u, ff_m) * 3 + piece + 1)
                    nc.scalar.activation(fuse_hi[:, 2 * piece:2 * piece + 2, :], fuse_part(u, ff_m, piece), ACT.Copy)\
                        .then_inc(fuse_hi_ready, 1)

            def values_high(u, k):
                m, j = divmod(k, GROUPS)
                par, nxt = m % 2, (m + 1) % 2
                if j == 3 and is_tile(u, m + 1):
                    act.wait_ge(kv_made["v_ctx"], tile(u, m + 1) + 1)
                    for c in range(2):
                        last = nc.scalar.activation(v_hi[c * LEN:(c + 1) * LEN, nxt, 1 - c, :],
                                                    kv_bank(u, m + 1, 2)[c * LEN:(c + 1) * LEN, :], ACT.Copy)
                    last.then_inc(vc_hi_ready, 1)
                if j == 0 and is_tile(u, m):
                    act.wait_ge(kv_made["v_self"], tile(u, m) + 1)
                    for r in range(2):
                        last = nc.scalar.activation(v_hi[r * LEN:(r + 1) * LEN, par, r, :],
                                                    kv_bank(u, m, 3)[r * LEN:(r + 1) * LEN, :], ACT.Copy)
                    last.then_inc(vs_hi_ready, 1)

            def square_queries(u, k):
                m, j = divmod(k, GROUPS)
                par, nxt = m % 2, (m + 1) % 2
                if is_step(u, k + 1):
                    act.wait_ge(q_made, step(u, k + 1) + 1)
                    if is_step(u, k):
                        act.wait_ge(ssq_moved, step(u, k) + 1)
                    if j == 1 and is_tile(u, m + 1):
                        act.wait_ge(kc_squared, tile(u, m + 1) + 1)
                    if j == 3 and is_tile(u, m + 1):
                        act.wait_ge(ks_squared, tile(u, m + 1) + 1)
                    square_heads(ps_q, ssq).then_inc(q_squared, 1)

            def tanh_gate(u, piece, ff_m):
                if is_tile(u, ff_m) and piece is not None:
                    act.wait_ge(ff_made, tile(u, ff_m) * 3 + piece + 1)
                    if isinstance(u, int) and tile(u, ff_m) == 0 and piece == 0:
                        act.wait_ge(scales_ready, 2)
                    for i in range(2):
                        c = 2 * piece + i
                        last = nc.scalar.activation(tanh_part(u, ff_m, piece)[:, i, :],
                                                    ff_bank(u, ff_m, piece)[:, i * P:(i + 1) * P], ACT.Tanh,
                                                    scale=tanh_scale[:, c:c + 1])
                    last.then_inc(tanh_ready, 1)

            def one_step(u, k):
                m, j = divmod(k, GROUPS)
                par, nxt = m % 2, (m + 1) % 2

                if is_step(u, k - 2):
                    act.wait_ge(attn_made, step(u, k - 2) + 1)
                    nc.scalar.activation(ot_hi[:, :, :].rearrange("p h (r l) -> p r h l", r=2),
                                         ps_o[:, :].rearrange("p (r h l) -> p r h l", r=2, h=HPG), ACT.Copy)\
                        .then_inc(ot_hi_ready, 1)

                if is_step(u, k):
                    act.wait_ge(q_turned, step(u, k) + 1)
                    nc.scalar.activation(qt[:, :, :, :], ps_t[:, :].rearrange("p (h r l) -> p r h l", h=HPG, r=2),
                                         ACT.Copy).then_inc(qt_ready, 1)

                if j == 1 and is_tile(u, m + 1):
                    t1 = tile(u, m + 1)
                    act.wait_ge(kv_made["k_ctx"], t1 + 1)
                    if is_step(u, k):
                        act.wait_ge(q_squared, step(u, k) + 1)
                    if isinstance(u, int) and t1 == 0:
                        act.wait_ge(tables_ready, 6)
                    if is_tile(u, m):
                        act.wait_ge(ks_var_ready, t1)
                    square_heads(kv_bank(u, m + 1, 0), k_ssq).then_inc(kc_squared, 1)

                piece, ff_m = piece_before(m, j)
                if not last_tile(u, ff_m):
                    tanh_gate(u, piece, ff_m)

                if at_step(u, k) == -1:
                    square_queries(u, k)
                    split_weights(u, k)
                    values_high(u, k)
                else:
                    values_high(u, k)
                    square_queries(u, k)

                after_last = isinstance(u, int) and step(u, k) >= STEPS
                if not after_last:
                    fuse_high(u, k)

                if at_step(u, k) == -2:
                    split_weights(u, k)

                if j == 2 and is_tile(u, m + 1):
                    t1 = tile(u, m + 1)
                    act.wait_ge(ks_roped, t1 + 1)
                    act.wait_ge(kc_var_ready, t1 + 1)
                    act.wait_ge(q_squared if is_step(u, k + 1) else kc_squared,
                                step(u, k + 1) + 1 if is_step(u, k + 1) else t1 + 1)
                    square_heads(kv_bank(u, m + 1, 1), k_ssq).then_inc(ks_squared, 1)

                if j == 0 and is_tile(u, m + 1):
                    act.wait_ge(xc_turned, tile(u, m + 1) + 1)
                    nc.scalar.activation(xt[0][:, nxt, :, :], four(ps_t), ACT.Copy).then_inc(xt_hi_ready, 1)
                if j == 2 and is_tile(u, m - 1):
                    act.wait_ge(x2_turned, tile(u, m - 1) + 1)
                    nc.scalar.activation(x2t[0][:, :, :].rearrange("p c n -> p (c n)"), ps_t[:, 0:HID], ACT.Copy)\
                        .then_inc(x2_hi_ready, 1)
                if j == 3 and is_tile(u, m + 1):
                    act.wait_ge(ks_turned, tile(u, m + 1) + 1)
                    nc.scalar.activation(kt[:, nxt, :, 0:4:3, :],
                                         ps_t[:, :].rearrange("p (g c m) -> p g c m", g=GROUPS, c=2), ACT.Copy)\
                        .then_inc(ks_stored, 1)

                if at_step(u, k) in (-4, -3):
                    split_weights(u, k)

                if is_step(u, k - 1):
                    act.wait_ge(probs_turned, step(u, k - 1) + 1)
                    nc.scalar.activation(pt_hi[:, :], ps_p[:, :], ACT.Copy).then_inc(pt_hi_ready, 1)

                piece, ff_m = piece_at(m, j)
                if last_tile(u, ff_m):
                    tanh_gate(u, piece, ff_m)
                if after_last:
                    fuse_high(u, k)

                if isinstance(u, int) and step(u, k) >= 0:
                    split_weights(u, k)

                if j == 1 and is_tile(u, m + 1):
                    act.wait_ge(kc_turned, tile(u, m + 1) + 1)
                    nc.scalar.activation(kt[:, nxt, :, 2:0:-1, :],
                                         ps_t[:, :].rearrange("p (g c m) -> p g c m", g=GROUPS, c=2), ACT.Copy,
                                         scale=k_w_col[:, 0:1]).then_inc(kc_stored, 1)

                if is_step(u, k):
                    act.wait_ge(bias_ready, step(u, k) + 1)
                    for i in range(4):
                        last = nc.scalar.activation(probs[:, i, :], ps_s[:, i * P:(i + 1) * P], ACT.Exp,
                                                    bias=exp_bias[:, i:i + 1], scale=q_scale[:, k % 2, i:i + 1],
                                                    accum_out=row_sum[:, i:i + 1])
                    last.then_inc(exp_ready, 1)

                if at_step(u, k) == -1:
                    act.wait_ge(late_in, 16 * 5)
                    nc.scalar.activation(tanh_gates[:, :], gates[:, :], ACT.Tanh).then_inc(gates_ready, 1)

            run_steps(act, one_step)

        @block.vector
        def _(dve):
            def as_f32(ap):
                return ap.bitcast(f32)

            def weight_lo(kind, i):
                n = CHUNKS.index((kind, i))
                dve.wait_ge(w_hi_ready, SPLIT_ORDER.index((kind, i)) + 1)
                hi, lo = {"kv": w_kv, "q": w_q}[kind]
                nc.vector.tensor_tensor(lo[:, i].rearrange("p c n -> p (c n)"), staged(n, CHUNK_COLS),
                                        as_f32(hi[:, i].rearrange("p c n -> p (c n)")), ALU.subtract)\
                    .then_inc(w_lo_ready, 1)

            def split_weights(u, k):
                for kind, i in SPLIT_AT.get(at_step(u, k), ()):
                    if (kind, i) == TABLES_AHEAD_OF:
                        tables()
                    if kind != "o":
                        weight_lo(kind, i)

            def rounding_constant(i):
                n = CHUNKS.index(FF_CHUNKS[i])
                dve.wait_ge(chunk_in[n], 16)
                if i:
                    dve.wait_ge(quant_done, i)
                nc.vector.tensor_scalar(quant_m[:, :].bitcast(u32), staged(n, FF).bitcast(u32), EXPONENT_BITS, None,
                                        ALU.bitwise_and).then_inc(quant_exp, 1)
                dve.wait_ge(quant_exp, i + 1)
                nc.vector.tensor_scalar(quant_m[:, :], quant_m[:, :], E4M3_MIN_NORMAL, E4M3_ROUNDER,
                                        ALU.max, ALU.mult).then_inc(quant_round, 1)

            def round_weights(i):
                n = CHUNKS.index(FF_CHUNKS[i])
                dve.wait_ge(quant_round, i + 1)
                nc.vector.tensor_tensor(staged(n, FF), staged(n, FF), quant_m[:, :], ALU.add).then_inc(quant_sum, 1)
                dve.wait_ge(quant_sum, i + 1)
                nc.vector.tensor_tensor(staged(n, FF), staged(n, FF), quant_m[:, :], ALU.subtract)\
                    .then_inc(quant_diff, 1)

            def out_of_range(i):
                n = CHUNKS.index(FF_CHUNKS[i])
                dve.wait_ge(quant_diff, i + 1)
                nc.vector.tensor_scalar(quant_m[:, :], staged(n, FF), E4M3_OVERFLOW, 0.0, ALU.mult, ALU.mult)\
                    .then_inc(quant_nan, 1)

            def tables():
                dve.wait_ge(const_in, 16)
                nc.vector.tensor_copy(mask[:, :], const[:, C_MASK:C_MASK + LEN]).then_inc(tables_ready, 1)
                nc.vector.tensor_copy(ident_bf[:, :], ident).then_inc(tables_ready, 1)
                dve.wait_ge(small_in, 16 * 7)
                for n in range(4):
                    col = C_COS if n % 2 == 0 else C_SIN
                    nc.vector.tensor_tensor(rope[:, n, :], const[:, col:col + DIM], rope[:, n, :], ALU.mult)\
                        .then_inc(tables_ready, 1)
            def scales():
                dve.wait_ge(scales_turned, 1)
                nc.vector.tensor_copy(ff_scales[:, :, :].rearrange("p a c -> p (a c)"), ps_y[:, 0:2 * FC])\
                    .then_inc(scales_copied, 1)
                dve.wait_ge(scales_copied, 1)
                nc.vector.tensor_scalar(tanh_scale[:, :], ff_scales[:, 0, :], 0.5 / FF_IN_SCALE, None, ALU.mult)\
                    .then_inc(scales_ready, 1)
                nc.vector.scalar_tensor_tensor(fuse_scale[:, :], ff_scales[:, 0, :], 0.5 / FF_IN_SCALE ** 2,
                                               ff_scales[:, 1, :], ALU.mult, ALU.mult).then_inc(scales_ready, 1)

            def down_row_scale():
                dve.wait_ge(gates_ready, 1)
                nc.vector.tensor_scalar(down_rows[:, :], down_rows[:, :], tanh_gates[:, 1:2], None, ALU.mult)\
                    .then_inc(scales_ready, 1)

            def x_tile(u, m):
                if isinstance(u, int):
                    return x_sb[:, tile(u, m), :]
                return x_sb[:, bass.ds(tile(u, m), 1), :].rearrange("p a n -> p (a n)")

            def values_low(u, k):
                m, j = divmod(k, GROUPS)
                par, nxt = m % 2, (m + 1) % 2
                if j == 3 and is_tile(u, m + 1):
                    dve.wait_ge(vc_hi_ready, tile(u, m + 1) + 1)
                    for c in range(2):
                        rows = slice(c * LEN, (c + 1) * LEN)
                        last = nc.vector.tensor_tensor(v_lo[rows, nxt, 1 - c, :], kv_bank(u, m + 1, 2)[rows, :],
                                                       as_f32(v_hi[rows, nxt, 1 - c, :]), ALU.subtract)
                    last.then_inc(vc_lo_ready, 1)
                if j == 0 and is_tile(u, m):
                    dve.wait_ge(vs_hi_ready, tile(u, m) + 1)
                    for r in range(2):
                        rows = slice(r * LEN, (r + 1) * LEN)
                        last = nc.vector.tensor_tensor(v_lo[rows, par, r, :], kv_bank(u, m, 3)[rows, :],
                                                       as_f32(v_hi[rows, par, r, :]), ALU.subtract)
                    last.then_inc(vs_lo_ready, 1)

            def rotate_queries(u, k):
                m, j = divmod(k, GROUPS)
                par, nxt = m % 2, (m + 1) % 2
                if is_step(u, k + 1):
                    dve.wait_ge(q_squared, step(u, k + 1) + 1)
                    if is_step(u, k):
                        dve.wait_ge(q_turned, step(u, k) + 1)
                    nc.vector.tensor_tensor(q_rot[:, :, :], four(ps_q), over_heads(rope[:, 0, :]), ALU.mult)\
                        .then_inc(q_cos_ready, 1)
                    if is_step(u, k):
                        dve.wait_ge(q_rot_ready, step(u, k) + 1)
                    nc.vector.tensor_tensor(halves(q_sin[:, :, :]), rotated(four(ps_q)), halves(over_heads(rope[:, 1, :])),
                                            ALU.mult).then_inc(q_sin_ready, 1)

            def attention_low(u, k):
                if is_step(u, k - 2):
                    dve.wait_ge(ot_hi_ready, step(u, k - 2) + 1)
                    nc.vector.tensor_tensor(ot_lo[:, :, :].rearrange("p h (r l) -> p r h l", r=2),
                                            ps_o[:, :].rearrange("p (r h l) -> p r h l", r=2, h=HPG),
                                            as_f32(ot_hi[:, :, :]).rearrange("p h (r l) -> p r h l", r=2), ALU.subtract)\
                        .then_inc(ot_lo_ready, 1)

            def one_step(u, k):
                m, j = divmod(k, GROUPS)
                par, nxt = m % 2, (m + 1) % 2

                if at_step(u, k) not in SHORT_OF_VECTOR:
                    attention_low(u, k)

                if at_step(u, k) == -1:
                    rotate_queries(u, k)
                    split_weights(u, k)

                if j == 2 and is_tile(u, m - 1):
                    dve.wait_ge(x2_inv_ready, tile(u, m - 1) + 1)
                    if is_tile(u, m + 1):
                        dve.wait_ge(xc_turned, tile(u, m + 1) + 1)
                    nc.vector.tensor_scalar(x2n[:, :], x1[:, nxt, :], x2_mean[:, 0:1], x2_inv[:, 0:1],
                                            ALU.subtract, ALU.mult).then_inc(x2_ready, 1)

                if j == 3 and is_tile(u, m + 2):
                    dve.wait_ge(ln_inv_ready, tile(u, m + 2) + 1)
                    if is_tile(u, m + 1):
                        dve.wait_ge(xc_turned, tile(u, m + 1) + 1)
                    if is_tile(u, m - 1):
                        dve.wait_ge(x2_turned, tile(u, m - 1) + 1)
                    nc.vector.tensor_scalar(xn[:, :], x_tile(u, m + 2), ln_mean[:, 0:1], ln_inv[:, 0:1],
                                            ALU.subtract, ALU.mult).then_inc(xn_ready, 1)

                if j == 1 and is_tile(u, m + 1):
                    t1 = tile(u, m + 1)
                    dve.wait_ge(kc_squared, t1 + 1)
                    if is_tile(u, m):
                        dve.wait_ge(ks_inv_ready, t1)
                    nc.vector.tensor_scalar(k_var[:, :], k_ssq[:, :], 1.0 / DIM, RMS_EPS, ALU.mult, ALU.add)\
                        .then_inc(kc_var_ready, 1)

                piece, ff_m = piece_before(m, j)
                if is_tile(u, ff_m) and piece is not None:
                    count = tile(u, ff_m) * 3 + piece + 1
                    dve.wait_ge(tanh_ready, count)
                    gated = tanh_part(u, ff_m, piece)
                    nc.vector.scalar_tensor_tensor(gated.rearrange("p a n -> p (a n)"),
                                                   gated.rearrange("p a n -> p (a n)"), 1.0,
                                                   ff_bank(u, ff_m, piece)[:, 0:2 * P], ALU.add, ALU.mult).then_inc(gated_ready, 1)
                    dve.wait_ge(gated_ready, count)
                    if piece > 0 and not last_tile(u, ff_m):
                        dve.wait_ge(fuse_lo_ready, count - 1)
                    elif piece == 0 and is_tile(u, ff_m - 1):
                        dve.wait_ge(result_ready, tile(u, ff_m))
                    for i in range(2):
                        c = 2 * piece + i
                        last = nc.vector.scalar_tensor_tensor(fuse_part(u, ff_m, piece)[:, i, :], gated[:, i, :],
                                                              fuse_scale[:, c:c + 1],
                                                              ff_bank(u, ff_m, piece)[:, (2 + i) * P:(3 + i) * P],
                                                              ALU.mult, ALU.mult)
                    last.then_inc(fuse_ready, 1)
                if is_tile(u, ff_m) and piece is None:
                    dve.wait_ge(down_made, tile(u, ff_m) + 1)
                    dve.wait_ge(fuse_lo_ready, tile(u, ff_m) * 3 + 3)
                    nc.vector.tensor_tensor(down_y, ff_bank(u, ff_m, piece)[:, 0:HID], down_rows[:, :], ALU.mult)\
                        .then_inc(down_scaled, 1)

                if j == 2 and is_tile(u, m + 1):
                    t1 = tile(u, m + 1)
                    dve.wait_ge(kv_made["k_self"], t1 + 1)
                    dve.wait_ge(kc_turned, t1 + 1)
                    nc.vector.tensor_tensor(k_cos[:, :, :], four(kv_bank(u, m + 1, 1)), over_heads(rope[:, 2, :]), ALU.mult)
                    nc.vector.tensor_tensor(halves(k_sin[:, :, :]), rotated(four(kv_bank(u, m + 1, 1))),
                                            halves(over_heads(rope[:, 3, :])), ALU.mult).then_inc(ks_roped, 1)

                if j == 1 and is_tile(u, m + 1):
                    dve.wait_ge(kc_inv_ready, tile(u, m + 1) + 1)
                    if is_tile(u, m):
                        dve.wait_ge(ks_turned, tile(u, m) + 1)
                    nc.vector.tensor_tensor(kn[:, :, :], four(kv_bank(u, m + 1, 0)),
                                            k_inv[:, :].unsqueeze(2).broadcast_to([P, HPG, DIM]), ALU.mult).then_inc(kc_ready, 1)
                if at_step(u, k) != -1:
                    values_low(u, k)
                    rotate_queries(u, k)
                else:
                    values_low(u, k)

                if j == 2 and is_tile(u, m - 1):
                    dve.wait_ge(x2_hi_ready, tile(u, m - 1) + 1)
                    nc.vector.tensor_tensor(x2t[1][:, :, :].rearrange("p c n -> p (c n)"), ps_t[:, 0:HID],
                                            x2t[0][:, :, :].rearrange("p c n -> p (c n)"), ALU.subtract)\
                        .then_inc(x2_lo_ready, 1)

                if j == 0 and is_tile(u, m + 1):
                    dve.wait_ge(xt_hi_ready, tile(u, m + 1) + 1)
                    nc.vector.tensor_tensor(xt[1][:, nxt, :, :], four(ps_t), as_f32(xt[0][:, nxt, :, :]), ALU.subtract)\
                        .then_inc(xt_lo_ready, 1)
                if j == 2 and is_tile(u, m + 1):
                    dve.wait_ge(ks_squared, tile(u, m + 1) + 1)
                    dve.wait_ge(kc_inv_ready, tile(u, m + 1) + 1)
                    nc.vector.tensor_scalar(k_var[:, :], k_ssq[:, :], 1.0 / DIM, RMS_EPS, ALU.mult, ALU.add)\
                        .then_inc(ks_var_ready, 1)

                if at_step(u, k) in SHORT_OF_VECTOR:
                    attention_low(u, k)

                if is_step(u, k):
                    dve.wait_ge(scores_made, step(u, k) + 1)
                    nc.vector.tensor_reduce(row_max[:, :], four(ps_s), AX.X, ALU.max).then_inc(max_ready, 1)
                    dve.wait_ge(max_ready, step(u, k) + 1)
                    dve.wait_ge(q_scale_ready, step(u, k) + 1)
                    nc.vector.scalar_tensor_tensor(exp_bias[:, :], row_max[:, :], -1.0, q_scale[:, k % 2, :],
                                                   ALU.mult, ALU.mult).then_inc(bias_ready, 1)

                if is_step(u, k - 1):
                    dve.wait_ge(pt_hi_ready, step(u, k - 1) + 1)
                    nc.vector.tensor_tensor(pt_lo[:, :], ps_p[:, :], as_f32(pt_hi[:, :]), ALU.subtract)\
                        .then_inc(pt_lo_ready, 1)

                if j == 2 and is_tile(u, m + 2):
                    ln_count = tile(u, m + 2) + 1
                    if isinstance(u, int) and tile(u, m + 2) == 0:
                        dve.wait_ge(x0_in, 32)
                    if isinstance(u, int) and tile(u, m + 2) == 1:
                        dve.wait_ge(x_in, 32)
                    nc.vector.bn_stats(ln_stats[:, :], x_tile(u, m + 2)).then_inc(ln_counted, 1)
                    dve.wait_ge(ln_counted, ln_count)
                if j == 1 and is_tile(u, m - 1):
                    count = tile(u, m - 1) + 1
                    dve.wait_ge(y_made, step(u, k - 2) + 1)
                    dve.wait_ge(x1_free[nxt], (u + (m - 1) // 2 + 1) * 32)
                    nc.vector.scalar_tensor_tensor(x1[:, nxt, :], ps_y[:, 0:HID], tanh_gates[:, 0:1], x_tile(u, m - 1),
                                                   ALU.mult, ALU.add).then_inc(x1_ready, 1)
                    dve.wait_ge(x1_ready, count)
                    nc.vector.bn_stats(x2_stats[:, :], x1[:, nxt, :]).then_inc(x2_counted, 1)
                    dve.wait_ge(x2_counted, count)
                if is_step(u, k + 1):
                    if is_step(u, k):
                        dve.wait_ge(q_scale_ready, step(u, k) + 1)
                    for r in range(2):
                        for hh in range(2):
                            last = nc.vector.tensor_scalar(ssq_rows[hh * LEN:(hh + 1) * LEN, 2 * r:2 * r + 2],
                                                           ssq[r * LEN:(r + 1) * LEN, hh::2], DIM * RMS_EPS, None,
                                                           ALU.add)
                    last.then_inc(ssq_moved, 1)

                if j == 2 and is_tile(u, m + 2):
                    nc.vector.bn_aggr(ln_mean[:, :], ln_stats[:, :]).then_inc(ln_averaged, 1)
                    dve.wait_ge(ln_averaged, ln_count)
                    if is_tile(u, m + 1):
                        dve.wait_ge(ln_inv_ready, ln_count - 1)
                    nc.vector.tensor_scalar(ln_var[:, :], ln_mean[:, 1:2], LN_EPS, None, ALU.add).then_inc(ln_var_ready, 1)

                if j == 1 and is_tile(u, m - 1):
                    nc.vector.bn_aggr(x2_mean[:, :], x2_stats[:, :]).then_inc(x2_averaged, 1)
                    dve.wait_ge(x2_averaged, count)
                    if is_tile(u, m - 2):
                        dve.wait_ge(x2_inv_ready, count - 1)
                    nc.vector.tensor_scalar(x2_var[:, :], x2_mean[:, 1:2], LN_EPS, FF_IN_SCALE ** -2, ALU.add, ALU.mult)\
                        .then_inc(x2_var_ready, 1)

                if isinstance(u, int) and step(u, k) >= 0:
                    split_weights(u, k)

                if at_step(u, k) in ROUND_AT:
                    rounding_constant(ROUND_AT[step(u, k)])

                if at_step(u, k) == -1:
                    scales()
                if isinstance(u, int) and step(u, k) < -1:
                    split_weights(u, k)

                if is_step(u, k):
                    dve.wait_ge(exp_ready, step(u, k) + 1)
                    nc.vector.reciprocal(row_inv[:, :], row_sum[:, :]).then_inc(inv_ready, 1)

                if isinstance(u, int) and step(u, k) == 0:
                    down_row_scale()
                if at_step(u, k) in ROUND_AT:
                    round_weights(ROUND_AT[step(u, k)])

                if at_step(u, k) in ROUND_AT:
                    out_of_range(ROUND_AT[step(u, k)])

            run_steps(dve, one_step)

        @block.gpsimd
        def _(pool):
            def inverse_root(dst, src):
                return nc.gpsimd.tensor_tensor(dst, src, minus_half[:, 0:src.shape[1]], ALU.pow)

            def wo_lo(g):
                n = CHUNKS.index(("o", g))
                pool.wait_ge(wo_hi_ready, g + 1)
                nc.gpsimd.tensor_tensor(w_o[1][:, g].rearrange("p h n -> p (h n)"), staged(n, CHUNK_COLS),
                                        w_o[0][:, g].rearrange("p h n -> p (h n)").bitcast(f32), ALU.subtract)\
                    .then_inc(wo_lo_ready, 1)

            def quantize_store(i):
                kind, c = FF_CHUNKS[i]
                pool.wait_ge(quant_nan, i + 1)
                if kind == "down":
                    dst = w_down[:, c * (FC // 2):(c + 1) * (FC // 2), :].rearrange("p c n -> p (c n)")
                else:
                    dst = w_ff[:, ("gate", "up").index(kind), c, :]
                nc.gpsimd.tensor_tensor(dst, staged(CHUNKS.index(FF_CHUNKS[i]), FF), quant_m[:, :], ALU.add)\
                    .then_inc(quant_done, 1)

            def one_step(u, k):
                m, j = divmod(k, GROUPS)

                if j == 1 and is_tile(u, m + 1):
                    t1 = tile(u, m + 1)
                    pool.wait_ge(kc_var_ready, t1 + 1)
                    if is_tile(u, m):
                        pool.wait_ge(ks_ready, t1)
                    inverse_root(k_inv[:, :], k_var[:, :]).then_inc(kc_inv_ready, 1)

                piece, ff_m = piece_before(m, j)
                if is_tile(u, ff_m) and piece is not None:
                    count = tile(u, ff_m) * 3 + piece + 1
                    hi = fuse_hi[:, 2 * piece:2 * piece + 2, :]
                    pool.wait_ge(fuse_hi_ready, count)
                    nc.gpsimd.tensor_tensor(fuse_lo[:, 2 * piece:2 * piece + 2, :], fuse_part(u, ff_m, piece), hi.bitcast(f32),
                                            ALU.subtract).then_inc(fuse_lo_ready, 1)
                if is_tile(u, ff_m) and piece is None:
                    pool.wait_ge(down_scaled, tile(u, ff_m) + 1)
                    nc.gpsimd.tensor_tensor(x1[:, m % 2, :], down_y, x1[:, m % 2, :], ALU.add)\
                        .then_inc(result_ready, 1)

                if j == 2 and is_tile(u, m + 1):
                    t1 = tile(u, m + 1)
                    pool.wait_ge(ks_roped, t1 + 1)
                    nc.gpsimd.tensor_tensor(k_cos[:, :, :], k_cos[:, :, :], k_sin[:, :, :], ALU.add)\
                        .then_inc(ks_added, 1)

                if is_step(u, k + 1):
                    pool.wait_ge(q_sin_ready, step(u, k + 1) + 1)
                    nc.gpsimd.tensor_tensor(q_rot[:, :, :], q_rot[:, :, :], q_sin[:, :, :], ALU.add)\
                        .then_inc(q_rot_ready, 1)

                if isinstance(u, int) and step(u, k) < 2 * GROUPS and step(u, k - 1) in ROUND_AT:
                    quantize_store(ROUND_AT[step(u, k - 1)])

                if j == 2 and is_tile(u, m + 1):
                    t1 = tile(u, m + 1)
                    pool.wait_ge(ks_var_ready, t1 + 1)
                    pool.wait_ge(kc_ready, t1 + 1)
                    inverse_root(k_inv[:, :], k_var[:, :]).then_inc(ks_inv_ready, 1)
                    pool.wait_ge(ks_added, t1 + 1)
                    pool.wait_ge(ks_inv_ready, t1 + 1)
                    nc.gpsimd.tensor_tensor(kn[:, :, :], k_cos[:, :, :],
                                            k_inv[:, :].unsqueeze(2).broadcast_to([P, HPG, DIM]), ALU.mult)\
                        .then_inc(ks_ready, 1)

                if is_step(u, k + 1):
                    pool.wait_ge(ssq_moved, step(u, k + 1) + 1)
                    if is_step(u, k - 1):
                        pool.wait_ge(exp_ready, step(u, k - 1) + 1)
                    inverse_root(q_scale[:, (k + 1) % 2, :], ssq_rows[:, :]).then_inc(q_scale_ready, 1)

                if j == 2 and is_tile(u, m + 2):
                    pool.wait_ge(ln_var_ready, tile(u, m + 2) + 1)
                    if is_tile(u, m + 1):
                        pool.wait_ge(xn_ready, tile(u, m + 1) + 1)
                    inverse_root(ln_inv[:, :], ln_var[:, :]).then_inc(ln_inv_ready, 1)

                for kind, i in SPLIT_AT.get(at_step(u, k), ()):
                    if kind == "o":
                        wo_lo(i)

                if j == 1 and is_tile(u, m - 1):
                    pool.wait_ge(x2_var_ready, tile(u, m - 1) + 1)
                    if is_tile(u, m - 2):
                        pool.wait_ge(x2_ready, tile(u, m - 2) + 1)
                    inverse_root(x2_inv[:, :], x2_var[:, :]).then_inc(x2_inv_ready, 1)

                if is_step(u, k):
                    pool.wait_ge(inv_ready, step(u, k) + 1)
                    nc.gpsimd.tensor_tensor(probs[:, :, :], probs[:, :, :],
                                            row_inv[:, :].unsqueeze(2).broadcast_to([P, 4, P]), ALU.mult).then_inc(probs_ready, 1)

                if at_step(u, k) == 2 * GROUPS - 1 and step(u, k) in ROUND_AT:
                    quantize_store(ROUND_AT[step(u, k)])

            nc.gpsimd.memset(minus_half[:, :], -0.5).then_inc(half_set, 1)
            for i in range(2):
                nc.gpsimd.memset(x1[:, i, 0:1], 0.0).then_inc(x1_free[i], 32)
            pool.wait_ge(half_set, 1)
            run_steps(pool, one_step)


_INS = ["x", "ctx_2048", "g_xattn", "g_ffn", "L0_xattn_wq", "L0_xattn_wk", "L0_xattn_wv", "L0_xattn_wo",
        "L0_xattn_wk_ctx", "L0_xattn_wv_ctx", "L0_xattn_q_norm_w", "L0_xattn_k_norm_w", "L0_ffn_gate_w",
        "L0_ffn_up_w", "L0_ffn_down_w", "L0_ffn_gate_scale", "L0_ffn_up_scale", "L0_ffn_down_scale"]


def shape_constants():
    inv_freq = (1.0 / 10000.0 ** (np.arange(0, DIM, 2, dtype=np.float32) / DIM)).astype(np.float32)
    angles = np.outer(np.arange(LEN, dtype=np.float32), inv_freq)
    angles = np.concatenate([angles, angles], -1)
    sign = np.where(np.arange(DIM) < HALF, -1.0, 1.0).astype(np.float32)
    table = np.zeros((P, C_ALL), np.float32)
    table[:, C_COS:C_COS + DIM] = np.tile(np.cos(angles), (2, 1))
    table[:, C_SIN:C_SIN + DIM] = np.tile(np.sin(angles) * sign, (2, 1))
    late = np.arange(LEN)[None, :] > np.arange(LEN)[:, None]
    table[:, C_MASK:C_MASK + LEN] = np.tile(np.where(late, MASKED, 0.0), (2, 1))
    table[:, C_ID:C_ID + P] = np.eye(P)
    return table


def kernel(**inputs):
    import concourse.bacc as bacc
    from concourse.bass_utils import run_bass_kernel_spmd

    nc = bacc.Bacc("TRN2", target_bir_lowering=False, num_devices=1)
    arrays, args = {}, []
    given = [(name, np.ascontiguousarray(inputs[name])) for name in _INS] + [("constants", shape_constants())]
    for name, a in given:
        arrays[f"in_{name}_dram"] = a
        args.append(nc.dram_tensor(f"in_{name}_dram", a.shape, mybir.dt.from_np(a.dtype), kind="ExternalInput").ap())
    args.append(nc.dram_tensor("out_0_dram", (BATCHES, LEN, HID), mybir.dt.float32, kind="ExternalOutput").ap())
    build(nc, *args)
    r = run_bass_kernel_spmd(nc, [arrays], core_ids=[0])
    return r.results[0]["out_0_dram"]
```
